# Optimizing a Trainium2 kernel written in Bass

```python
import numpy as np
import jax
import jax.numpy as jnp

def _softmax(x, axis=-1):
    return jax.nn.softmax(x, axis=axis)

def _gelu(x):
    return jax.nn.gelu(x, approximate=True)

def _silu(x):
    return jax.nn.silu(x)

def _sigmoid(x):
    return jax.nn.sigmoid(x)

def _layernorm(x, axis=-1, eps=1e-05):
    m = jnp.mean(x, axis=axis, keepdims=True)
    v = jnp.var(x, axis=axis, keepdims=True)
    return (x - m) / jnp.sqrt(v + eps)

def _scatter_add(tgt, idx, src, axis=0):
    return tgt.at[idx].add(src)

def _segment_sum(src, seg, n):
    return jax.ops.segment_sum(src, seg, n)
kernel_name = 'mk_dlrm_tower_d1_rec_r8_791024'

def setup_inputs(seed: int=0):
    np.random.seed(seed)
    _w = jnp.asarray

    def _rec_inputs():
        import jax
        import jax.numpy as jnp
        _tk = jax.random.key(seed)
        dense_ctx = jax.random.normal(jax.random.fold_in(_tk, 190), (512, 16), jnp.float32)
        ids = jnp.stack([jax.random.randint(jax.random.fold_in(_tk, 200 + f), (512,), 0, v, jnp.int32) for f, v in enumerate([12500, 1000, 1000, 125000, 12500, 1250, 12500, 125000, 1000, 1250, 125000, 12500, 1250, 125000, 1250, 1000, 1250, 1250, 12500, 1000, 12500, 12500, 12500, 125000, 1250, 12500, 125000, 1000, 1250, 1000, 125000, 1250, 125000, 12500, 125000, 1000, 1250, 1000, 12500, 12500, 1250, 125000, 125000, 12500, 1250, 1000, 12500, 125000, 12500, 1000, 125000, 12500, 12500, 1000, 12500, 1250, 1000, 1000, 1000, 1250, 12500, 1250, 1250, 1000])], axis=1)
        tbl_0 = 0.05 * jax.random.normal(jax.random.fold_in(_tk, 500 + 0), (12500, 16), jnp.float32)
        tbl_1 = 0.05 * jax.random.normal(jax.random.fold_in(_tk, 500 + 1), (1000, 16), jnp.float32)
        tbl_2 = 0.05 * jax.random.normal(jax.random.fold_in(_tk, 500 + 2), (1000, 16), jnp.float32)
        tbl_3 = 0.05 * jax.random.normal(jax.random.fold_in(_tk, 500 + 3), (125000, 16), jnp.float32)
        tbl_4 = 0.05 * jax.random.normal(jax.random.fold_in(_tk, 500 + 4), (12500, 16), jnp.float32)
        tbl_5 = 0.05 * jax.random.normal(jax.random.fold_in(_tk, 500 + 5), (1250, 16), jnp.float32)
        tbl_6 = 0.05 * jax.random.normal(jax.random.fold_in(_tk, 500 + 6), (12500, 16), jnp.float32)
        tbl_7 = 0.05 * jax.random.normal(jax.random.fold_in(_tk, 500 + 7), (125000, 16), jnp.float32)
        tbl_8 = 0.05 * jax.random.normal(jax.random.fold_in(_tk, 500 + 8), (1000, 16), jnp.float32)
        tbl_9 = 0.05 * jax.random.normal(jax.random.fold_in(_tk, 500 + 9), (1250, 16), jnp.float32)
        tbl_10 = 0.05 * jax.random.normal(jax.random.fold_in(_tk, 500 + 10), (125000, 16), jnp.float32)
        tbl_11 = 0.05 * jax.random.normal(jax.random.fold_in(_tk, 500 + 11), (12500, 16), jnp.float32)
        tbl_12 = 0.05 * jax.random.normal(jax.random.fold_in(_tk, 500 + 12), (1250, 16), jnp.float32)
        tbl_13 = 0.05 * jax.random.normal(jax.random.fold_in(_tk, 500 + 13), (125000, 16), jnp.float32)
        tbl_14 = 0.05 * jax.random.normal(jax.random.fold_in(_tk, 500 + 14), (1250, 16), jnp.float32)
        tbl_15 = 0.05 * jax.random.normal(jax.random.fold_in(_tk, 500 + 15), (1000, 16), jnp.float32)
        tbl_16 = 0.05 * jax.random.normal(jax.random.fold_in(_tk, 500 + 16), (1250, 16), jnp.float32)
        tbl_17 = 0.05 * jax.random.normal(jax.random.fold_in(_tk, 500 + 17), (1250, 16), jnp.float32)
        tbl_18 = 0.05 * jax.random.normal(jax.random.fold_in(_tk, 500 + 18), (12500, 16), jnp.float32)
        tbl_19 = 0.05 * jax.random.normal(jax.random.fold_in(_tk, 500 + 19), (1000, 16), jnp.float32)
        tbl_20 = 0.05 * jax.random.normal(jax.random.fold_in(_tk, 500 + 20), (12500, 16), jnp.float32)
        tbl_21 = 0.05 * jax.random.normal(jax.random.fold_in(_tk, 500 + 21), (12500, 16), jnp.float32)
        tbl_22 = 0.05 * jax.random.normal(jax.random.fold_in(_tk, 500 + 22), (12500, 16), jnp.float32)
        tbl_23 = 0.05 * jax.random.normal(jax.random.fold_in(_tk, 500 + 23), (125000, 16), jnp.float32)
        tbl_24 = 0.05 * jax.random.normal(jax.random.fold_in(_tk, 500 + 24), (1250, 16), jnp.float32)
        tbl_25 = 0.05 * jax.random.normal(jax.random.fold_in(_tk, 500 + 25), (12500, 16), jnp.float32)
        tbl_26 = 0.05 * jax.random.normal(jax.random.fold_in(_tk, 500 + 26), (125000, 16), jnp.float32)
        tbl_27 = 0.05 * jax.random.normal(jax.random.fold_in(_tk, 500 + 27), (1000, 16), jnp.float32)
        tbl_28 = 0.05 * jax.random.normal(jax.random.fold_in(_tk, 500 + 28), (1250, 16), jnp.float32)
        tbl_29 = 0.05 * jax.random.normal(jax.random.fold_in(_tk, 500 + 29), (1000, 16), jnp.float32)
        tbl_30 = 0.05 * jax.random.normal(jax.random.fold_in(_tk, 500 + 30), (125000, 16), jnp.float32)
        tbl_31 = 0.05 * jax.random.normal(jax.random.fold_in(_tk, 500 + 31), (1250, 16), jnp.float32)
        tbl_32 = 0.05 * jax.random.normal(jax.random.fold_in(_tk, 500 + 32), (125000, 16), jnp.float32)
        tbl_33 = 0.05 * jax.random.normal(jax.random.fold_in(_tk, 500 + 33), (12500, 16), jnp.float32)
        tbl_34 = 0.05 * jax.random.normal(jax.random.fold_in(_tk, 500 + 34), (125000, 16), jnp.float32)
        tbl_35 = 0.05 * jax.random.normal(jax.random.fold_in(_tk, 500 + 35), (1000, 16), jnp.float32)
        tbl_36 = 0.05 * jax.random.normal(jax.random.fold_in(_tk, 500 + 36), (1250, 16), jnp.float32)
        tbl_37 = 0.05 * jax.random.normal(jax.random.fold_in(_tk, 500 + 37), (1000, 16), jnp.float32)
        tbl_38 = 0.05 * jax.random.normal(jax.random.fold_in(_tk, 500 + 38), (12500, 16), jnp.float32)
        tbl_39 = 0.05 * jax.random.normal(jax.random.fold_in(_tk, 500 + 39), (12500, 16), jnp.float32)
        tbl_40 = 0.05 * jax.random.normal(jax.random.fold_in(_tk, 500 + 40), (1250, 16), jnp.float32)
        tbl_41 = 0.05 * jax.random.normal(jax.random.fold_in(_tk, 500 + 41), (125000, 16), jnp.float32)
        tbl_42 = 0.05 * jax.random.normal(jax.random.fold_in(_tk, 500 + 42), (125000, 16), jnp.float32)
        tbl_43 = 0.05 * jax.random.normal(jax.random.fold_in(_tk, 500 + 43), (12500, 16), jnp.float32)
        tbl_44 = 0.05 * jax.random.normal(jax.random.fold_in(_tk, 500 + 44), (1250, 16), jnp.float32)
        tbl_45 = 0.05 * jax.random.normal(jax.random.fold_in(_tk, 500 + 45), (1000, 16), jnp.float32)
        tbl_46 = 0.05 * jax.random.normal(jax.random.fold_in(_tk, 500 + 46), (12500, 16), jnp.float32)
        tbl_47 = 0.05 * jax.random.normal(jax.random.fold_in(_tk, 500 + 47), (125000, 16), jnp.float32)
        tbl_48 = 0.05 * jax.random.normal(jax.random.fold_in(_tk, 500 + 48), (12500, 16), jnp.float32)
        tbl_49 = 0.05 * jax.random.normal(jax.random.fold_in(_tk, 500 + 49), (1000, 16), jnp.float32)
        tbl_50 = 0.05 * jax.random.normal(jax.random.fold_in(_tk, 500 + 50), (125000, 16), jnp.float32)
        tbl_51 = 0.05 * jax.random.normal(jax.random.fold_in(_tk, 500 + 51), (12500, 16), jnp.float32)
        tbl_52 = 0.05 * jax.random.normal(jax.random.fold_in(_tk, 500 + 52), (12500, 16), jnp.float32)
        tbl_53 = 0.05 * jax.random.normal(jax.random.fold_in(_tk, 500 + 53), (1000, 16), jnp.float32)
        tbl_54 = 0.05 * jax.random.normal(jax.random.fold_in(_tk, 500 + 54), (12500, 16), jnp.float32)
        tbl_55 = 0.05 * jax.random.normal(jax.random.fold_in(_tk, 500 + 55), (1250, 16), jnp.float32)
        tbl_56 = 0.05 * jax.random.normal(jax.random.fold_in(_tk, 500 + 56), (1000, 16), jnp.float32)
        tbl_57 = 0.05 * jax.random.normal(jax.random.fold_in(_tk, 500 + 57), (1000, 16), jnp.float32)
        tbl_58 = 0.05 * jax.random.normal(jax.random.fold_in(_tk, 500 + 58), (1000, 16), jnp.float32)
        tbl_59 = 0.05 * jax.random.normal(jax.random.fold_in(_tk, 500 + 59), (1250, 16), jnp.float32)
        tbl_60 = 0.05 * jax.random.normal(jax.random.fold_in(_tk, 500 + 60), (12500, 16), jnp.float32)
        tbl_61 = 0.05 * jax.random.normal(jax.random.fold_in(_tk, 500 + 61), (1250, 16), jnp.float32)
        tbl_62 = 0.05 * jax.random.normal(jax.random.fold_in(_tk, 500 + 62), (1250, 16), jnp.float32)
        tbl_63 = 0.05 * jax.random.normal(jax.random.fold_in(_tk, 500 + 63), (1000, 16), jnp.float32)
        _rk = jax.random.fold_in(_tk, 7)
        W_top1 = 0.05 * jax.random.normal(jax.random.fold_in(_tk, 801), (400, 512), jnp.float32)
        W_top2 = 0.0441942 * jax.random.normal(jax.random.fold_in(_tk, 802), (512, 256), jnp.float32)
        W_top3 = 0.0625 * jax.random.normal(jax.random.fold_in(_tk, 803), (256, 1), jnp.float32)
        b_top1 = jnp.zeros((512,), jnp.float32)
        b_top2 = jnp.zeros((256,), jnp.float32)
        return (dense_ctx, ids, tbl_0, tbl_1, tbl_2, tbl_3, tbl_4, tbl_5, tbl_6, tbl_7, tbl_8, tbl_9, tbl_10, tbl_11, tbl_12, tbl_13, tbl_14, tbl_15, tbl_16, tbl_17, tbl_18, tbl_19, tbl_20, tbl_21, tbl_22, tbl_23, tbl_24, tbl_25, tbl_26, tbl_27, tbl_28, tbl_29, tbl_30, tbl_31, tbl_32, tbl_33, tbl_34, tbl_35, tbl_36, tbl_37, tbl_38, tbl_39, tbl_40, tbl_41, tbl_42, tbl_43, tbl_44, tbl_45, tbl_46, tbl_47, tbl_48, tbl_49, tbl_50, tbl_51, tbl_52, tbl_53, tbl_54, tbl_55, tbl_56, tbl_57, tbl_58, tbl_59, tbl_60, tbl_61, tbl_62, tbl_63, W_top1, b_top1, W_top2, b_top2, W_top3)
    dense_ctx, ids, tbl_0, tbl_1, tbl_2, tbl_3, tbl_4, tbl_5, tbl_6, tbl_7, tbl_8, tbl_9, tbl_10, tbl_11, tbl_12, tbl_13, tbl_14, tbl_15, tbl_16, tbl_17, tbl_18, tbl_19, tbl_20, tbl_21, tbl_22, tbl_23, tbl_24, tbl_25, tbl_26, tbl_27, tbl_28, tbl_29, tbl_30, tbl_31, tbl_32, tbl_33, tbl_34, tbl_35, tbl_36, tbl_37, tbl_38, tbl_39, tbl_40, tbl_41, tbl_42, tbl_43, tbl_44, tbl_45, tbl_46, tbl_47, tbl_48, tbl_49, tbl_50, tbl_51, tbl_52, tbl_53, tbl_54, tbl_55, tbl_56, tbl_57, tbl_58, tbl_59, tbl_60, tbl_61, tbl_62, tbl_63, W_top1, b_top1, W_top2, b_top2, W_top3 = _rec_inputs()

    def _L0_rec_setup():
        import jax, jax.numpy as jnp
        import numpy as np
        B, F0, D = (256, 64, 16)
        CIN_SIZES = [128, 128, 128]

        def _cin_layer(x0, xi, W):
            F0_, Fi, Fn = (x0.shape[1], xi.shape[1], W.shape[-1])
            Wr = W.reshape(F0_, Fi, Fn)
            return jnp.einsum('bid,bjd,ijn->bnd', x0, xi, Wr)
        key = jax.random.key(seed)
        ks = jax.random.split(key, 4)
        x = jax.random.normal(ks[0], (B, F0, D), dtype=jnp.float32)
        field_nums = [F0] + CIN_SIZES
        Ws = []
        for i in range(len(CIN_SIZES)):
            fan_in = F0 * field_nums[i]
            fan_out = field_nums[i + 1]
            limit = np.sqrt(6.0 / (fan_in + fan_out)).astype(np.float32)
            W = jax.random.uniform(ks[i + 1], (fan_in, fan_out), dtype=jnp.float32, minval=-limit, maxval=limit)
            Ws.append(W)
        return {'x': x, 'W0': Ws[0], 'W1': Ws[1], 'W2': Ws[2]}
    _L0_rec_all = _L0_rec_setup()
    _L0_rec_in = {k: v for k, v in _L0_rec_all.items() if k in ('W0', 'W1', 'W2')}
    del _L0_rec_all
    return {'dense_ctx': dense_ctx, 'ids': ids, 'tbl_0': tbl_0, 'tbl_1': tbl_1, 'tbl_2': tbl_2, 'tbl_3': tbl_3, 'tbl_4': tbl_4, 'tbl_5': tbl_5, 'tbl_6': tbl_6, 'tbl_7': tbl_7, 'tbl_8': tbl_8, 'tbl_9': tbl_9, 'tbl_10': tbl_10, 'tbl_11': tbl_11, 'tbl_12': tbl_12, 'tbl_13': tbl_13, 'tbl_14': tbl_14, 'tbl_15': tbl_15, 'tbl_16': tbl_16, 'tbl_17': tbl_17, 'tbl_18': tbl_18, 'tbl_19': tbl_19, 'tbl_20': tbl_20, 'tbl_21': tbl_21, 'tbl_22': tbl_22, 'tbl_23': tbl_23, 'tbl_24': tbl_24, 'tbl_25': tbl_25, 'tbl_26': tbl_26, 'tbl_27': tbl_27, 'tbl_28': tbl_28, 'tbl_29': tbl_29, 'tbl_30': tbl_30, 'tbl_31': tbl_31, 'tbl_32': tbl_32, 'tbl_33': tbl_33, 'tbl_34': tbl_34, 'tbl_35': tbl_35, 'tbl_36': tbl_36, 'tbl_37': tbl_37, 'tbl_38': tbl_38, 'tbl_39': tbl_39, 'tbl_40': tbl_40, 'tbl_41': tbl_41, 'tbl_42': tbl_42, 'tbl_43': tbl_43, 'tbl_44': tbl_44, 'tbl_45': tbl_45, 'tbl_46': tbl_46, 'tbl_47': tbl_47, 'tbl_48': tbl_48, 'tbl_49': tbl_49, 'tbl_50': tbl_50, 'tbl_51': tbl_51, 'tbl_52': tbl_52, 'tbl_53': tbl_53, 'tbl_54': tbl_54, 'tbl_55': tbl_55, 'tbl_56': tbl_56, 'tbl_57': tbl_57, 'tbl_58': tbl_58, 'tbl_59': tbl_59, 'tbl_60': tbl_60, 'tbl_61': tbl_61, 'tbl_62': tbl_62, 'tbl_63': tbl_63, 'W_top1': W_top1, 'b_top1': b_top1, 'W_top2': W_top2, 'b_top2': b_top2, 'W_top3': W_top3, 'L0_rec_W0': _L0_rec_in['W0'], 'L0_rec_W1': _L0_rec_in['W1'], 'L0_rec_W2': _L0_rec_in['W2']}

def reference(dense_ctx, ids, tbl_0, tbl_1, tbl_2, tbl_3, tbl_4, tbl_5, tbl_6, tbl_7, tbl_8, tbl_9, tbl_10, tbl_11, tbl_12, tbl_13, tbl_14, tbl_15, tbl_16, tbl_17, tbl_18, tbl_19, tbl_20, tbl_21, tbl_22, tbl_23, tbl_24, tbl_25, tbl_26, tbl_27, tbl_28, tbl_29, tbl_30, tbl_31, tbl_32, tbl_33, tbl_34, tbl_35, tbl_36, tbl_37, tbl_38, tbl_39, tbl_40, tbl_41, tbl_42, tbl_43, tbl_44, tbl_45, tbl_46, tbl_47, tbl_48, tbl_49, tbl_50, tbl_51, tbl_52, tbl_53, tbl_54, tbl_55, tbl_56, tbl_57, tbl_58, tbl_59, tbl_60, tbl_61, tbl_62, tbl_63, W_top1, b_top1, W_top2, b_top2, W_top3, L0_rec_W0, L0_rec_W1, L0_rec_W2):
    import jax
    import jax.numpy as jnp

    def _L0_rec_ref(x, W0, W1, W2):
        import jax, jax.numpy as jnp
        import numpy as np
        B, F0, D = (256, 64, 16)
        CIN_SIZES = [128, 128, 128]

        def _cin_layer(x0, xi, W):
            F0_, Fi, Fn = (x0.shape[1], xi.shape[1], W.shape[-1])
            Wr = W.reshape(F0_, Fi, Fn)
            return jnp.einsum('bid,bjd,ijn->bnd', x0, xi, Wr)
        h = x
        outs = []
        for W in (W0, W1, W2):
            h = _cin_layer(x, h, W)
            outs.append(h)
        res = jnp.concatenate(outs, axis=1)
        return jnp.sum(res, axis=-1)
    e = jnp.stack([tbl_0[ids[:, 0]], tbl_1[ids[:, 1]], tbl_2[ids[:, 2]], tbl_3[ids[:, 3]], tbl_4[ids[:, 4]], tbl_5[ids[:, 5]], tbl_6[ids[:, 6]], tbl_7[ids[:, 7]], tbl_8[ids[:, 8]], tbl_9[ids[:, 9]], tbl_10[ids[:, 10]], tbl_11[ids[:, 11]], tbl_12[ids[:, 12]], tbl_13[ids[:, 13]], tbl_14[ids[:, 14]], tbl_15[ids[:, 15]], tbl_16[ids[:, 16]], tbl_17[ids[:, 17]], tbl_18[ids[:, 18]], tbl_19[ids[:, 19]], tbl_20[ids[:, 20]], tbl_21[ids[:, 21]], tbl_22[ids[:, 22]], tbl_23[ids[:, 23]], tbl_24[ids[:, 24]], tbl_25[ids[:, 25]], tbl_26[ids[:, 26]], tbl_27[ids[:, 27]], tbl_28[ids[:, 28]], tbl_29[ids[:, 29]], tbl_30[ids[:, 30]], tbl_31[ids[:, 31]], tbl_32[ids[:, 32]], tbl_33[ids[:, 33]], tbl_34[ids[:, 34]], tbl_35[ids[:, 35]], tbl_36[ids[:, 36]], tbl_37[ids[:, 37]], tbl_38[ids[:, 38]], tbl_39[ids[:, 39]], tbl_40[ids[:, 40]], tbl_41[ids[:, 41]], tbl_42[ids[:, 42]], tbl_43[ids[:, 43]], tbl_44[ids[:, 44]], tbl_45[ids[:, 45]], tbl_46[ids[:, 46]], tbl_47[ids[:, 47]], tbl_48[ids[:, 48]], tbl_49[ids[:, 49]], tbl_50[ids[:, 50]], tbl_51[ids[:, 51]], tbl_52[ids[:, 52]], tbl_53[ids[:, 53]], tbl_54[ids[:, 54]], tbl_55[ids[:, 55]], tbl_56[ids[:, 56]], tbl_57[ids[:, 57]], tbl_58[ids[:, 58]], tbl_59[ids[:, 59]], tbl_60[ids[:, 60]], tbl_61[ids[:, 61]], tbl_62[ids[:, 62]], tbl_63[ids[:, 63]]], axis=1)
    z = _L0_rec_ref(e, L0_rec_W0, L0_rec_W1, L0_rec_W2)
    z = z.reshape(z.shape[0], -1)
    h = jnp.concatenate([z, dense_ctx], axis=1)
    h = jnp.maximum(h @ W_top1 + b_top1, 0.0)
    h = jnp.maximum(h @ W_top2 + b_top2, 0.0)
    y = h @ W_top3
    return y

_drawn_inputs = setup_inputs


def setup_inputs(seed=0):
    import zlib

    import numpy as np

    out = dict(_drawn_inputs(seed))
    spreads = {'b_top1': (0.0, 0.782), 'b_top2': (0.0, 0.341)}
    factors = {'tbl_0': 8.0,
     'tbl_1': 8.0,
     'tbl_2': 7.953,
     'tbl_3': 8.0,
     'tbl_4': 8.0,
     'tbl_5': 8.0,
     'tbl_6': 7.682,
     'tbl_7': 8.0,
     'tbl_8': 8.0,
     'tbl_9': 8.0,
     'tbl_10': 8.0,
     'tbl_11': 8.0,
     'tbl_12': 8.0,
     'tbl_13': 7.568,
     'tbl_14': 8.0,
     'tbl_15': 8.0,
     'tbl_16': 8.0,
     'tbl_17': 8.0,
     'tbl_18': 8.0,
     'tbl_19': 7.986,
     'tbl_20': 8.0,
     'tbl_21': 8.0,
     'tbl_22': 8.0,
     'tbl_23': 8.0,
     'tbl_24': 8.0,
     'tbl_25': 8.0,
     'tbl_26': 7.963,
     'tbl_27': 8.0,
     'tbl_28': 8.0,
     'tbl_29': 8.0,
     'tbl_30': 8.0,
     'tbl_31': 8.0,
     'tbl_32': 7.534,
     'tbl_33': 8.0,
     'tbl_34': 8.0,
     'tbl_35': 8.0,
     'tbl_36': 8.0,
     'tbl_37': 8.0,
     'tbl_38': 7.99,
     'tbl_39': 8.0,
     'tbl_40': 8.0,
     'tbl_41': 7.805,
     'tbl_42': 8.0,
     'tbl_43': 8.0,
     'tbl_44': 8.0,
     'tbl_45': 8.0,
     'tbl_46': 8.0,
     'tbl_47': 8.0,
     'tbl_48': 8.0,
     'tbl_49': 8.0,
     'tbl_50': 8.0,
     'tbl_51': 8.0,
     'tbl_52': 8.0,
     'tbl_53': 8.0,
     'tbl_54': 8.0,
     'tbl_55': 8.0,
     'tbl_56': 8.0,
     'tbl_57': 8.0,
     'tbl_58': 8.0,
     'tbl_59': 8.0,
     'tbl_60': 8.0,
     'tbl_61': 8.0,
     'tbl_62': 8.0,
     'tbl_63': 8.0,
     'L0_rec_W1': 8.0,
     'L0_rec_W2': 8.0}
    for name, (base, spread) in spreads.items():
        noise = np.random.default_rng([zlib.crc32(name.encode()), seed]).standard_normal(out[name].shape)
        drawn = base * np.exp(spread * noise) if base else spread * noise
        out[name] = jnp.asarray(drawn.astype(out[name].dtype))
    for name, factor in factors.items():
        out[name] = (out[name] * factor).astype(out[name].dtype)
    return out
```

```python
from contextlib import ExitStack

import numpy as np

import concourse.bass as bass
from concourse import mybir

ALU = mybir.AluOpType
ACT = mybir.ActivationFunctionType
AX = mybir.AxisListType
F32 = mybir.dt.float32
F32R = mybir.dt.float32r
I32 = mybir.dt.int32

P = 128
B = 512
F = 64
D = 16
N = 128
FX = F + 1
BLOCKS = B // P
DQ = 4
GROUPS = BLOCKS * D // DQ
COLS = DQ * P

QUAD = 4
QUADS = F // QUAD
SLOTS = DQ * QUADS
YBANKS = 4

ROTA = 5
ROTB = 4
TILES0 = [(kb, a) for kb in range(ROTB) for a in range(ROTA if kb == 0 else ROTA - 1)]
NT0 = len(TILES0)
LAST_OF_KB = [max(n for n, (kb, _) in enumerate(TILES0) if kb == k) for k in range(ROTB)]
TT = ROTA + ROTB
TBANKS = 3
ZBUFS = 3

DVE_QUADS = [q for q in range(QUADS) if q % 2 == 0]
ACT_QUADS = [q for q in range(QUADS) if q % 2 == 1]
ND, NA = len(DVE_QUADS), len(ACT_QUADS)
ADDS = NA - 1
TMPS = 3

FOLD_AFTER = {DVE_QUADS[1]: 0, DVE_QUADS[3]: 1, DVE_QUADS[4]: 2}

EXT_SLOT = 3
EXTB_SLOT = [9, 17, 25, 35]
HIGH_SLOT = 5
LOW_SLOT = 10
EXTW = 2 * F + 8 * (ROTA - 1)
T_SLOT = [6, 8, 10, 12, 14, 16, 24, 33, 43]
L0_SLOT = [20 + (n * 19) // 8 for n in range(NT0)]
Z_SLOT = [s - 4 for s in L0_SLOT]
COPY_SLOT = {2: 0, 3: 1, 4: 2}
GATHERS = 16
HALF = B // 2


def quads_before(quads, slot):
    return slot // QUADS * len(quads) + sum(q < slot % QUADS for q in quads)


AHEAD_D = -quads_before(DVE_QUADS, 1 - YBANKS)
AHEAD_A = -quads_before(ACT_QUADS, 1 - YBANKS)


def halves_done(k, quads):
    return k * (2 * DQ * ND) + 2 * (quads + AHEAD_D)


def act_done(k, quads):
    return k * (DQ * NA) + (quads + AHEAD_A)


def tmp_slot(d, a):
    return (d * ADDS + a - 1) % TMPS


def dlrm(nc, tables, ids, id_base, w0a, w0b, w1, w2, dense, wt1, bt1, wt2, bt2, wt3, y):
    x_dram = nc.dram_tensor("x_scratch", (B, D * FX), F32, kind="Internal").ap()
    h1_dram = nc.dram_tensor("h1_scratch", (B, D * N), F32, kind="Internal").ap()
    with ExitStack() as ctx:
        def sb(name, shape, dt=F32):
            return ctx.enter_context(nc.sbuf_tensor(name, shape, dt))

        def sem(name):
            return ctx.enter_context(nc.semaphore(name))

        keep = {
            "w2": sb("w2", [P, F // 2, N]), "bd": sb("bd", [P, 16, 4 * FX]), "stack": sb("stack", [P, 16, N]),
            "h0sum": sb("h0sum", [P, B]), "ident": sb("ident", [P, P]),
            "dense": sb("dense_sb", [P, BLOCKS, D]), "wt1": sb("wt1", [P, 3, 512]), "wt1d": sb("wt1d", [D, 512]),
            "wt2": sb("wt2", [P, 4, 256]), "wt3": sb("wt3", [P, 2]), "bt1": sb("bt1", [P, 4]), "bt2": sb("bt2", [P, 2]),
        }
        tail_loaded = sem("tail_loaded")
        cin_layers_0_1(nc, keep, tail_loaded, x_dram, h1_dram, tables, ids, id_base, w0a, w0b, w1, w2,
                       dense, wt1, bt1, wt2, bt2, wt3)
        layer_2_and_mlp(nc, keep, tail_loaded, x_dram, h1_dram, w2, y)


def cin_layers_0_1(nc, keep, tail_loaded, x_dram, h1_dram, tables, ids, id_base, w0a, w0b, w1, w2,
                   dense, wt1, bt1, wt2, bt2, wt3):
    with ExitStack() as ctx:
        def sb(name, shape, dt=F32):
            return ctx.enter_context(nc.sbuf_tensor(name, shape, dt))

        def psum(name, shape):
            return ctx.enter_context(nc.psum_tensor(name, shape, F32))

        def sem(name):
            return ctx.enter_context(nc.semaphore(name))

        w2_sb, bd, ident, h0sum = keep["w2"], keep["bd"], keep["ident"], keep["h0sum"]
        w1_hi = sb("w1_hi", [P, F * N], F32R)
        w1_lo = sb("w1_lo", [P, F * N], F32R)
        w0 = sb("w0", [P, NT0, N])
        xp = sb("xp", [P, BLOCKS * D, FX])
        ids_sb = sb("ids_sb", [P, BLOCKS * F], I32)
        base_sb = sb("base_sb", [P, F], I32)
        idx = sb("idx", [P, BLOCKS * F], I32)
        idx_now = sb("idx_now", [P, GATHERS], I32)
        raw0 = sb("raw0", [P, F * D])
        raw = sb("raw", [P, GATHERS * D])
        ext = sb("ext", [P, DQ, EXTW])
        extb = sb("extb", [P, ROTB, DQ, P])
        xs = sb("xs", [P, DQ, F])
        rota = sb("rota", [P, ROTA, COLS])
        z = sb("z", [P, ZBUFS, COLS])
        h0_hi = sb("h0_hi", [P, COLS], F32R)
        h0_lo = sb("h0_lo", [P, COLS], F32R)
        h0part = sb("h0part", [P, P])
        tmp = sb("tmp", [P, TMPS, QUAD * N])
        acc_d = sb("acc_d", [P, 2, QUAD * N])
        acc_p = sb("acc_p", [P, 2, QUAD * N])
        h1 = sb("h1", [P, DQ, N])

        yq = psum("yq", [P, YBANKS, QUAD * N])
        l0acc = psum("l0acc", [P, COLS])
        tb = psum("tb", [P, TBANKS, COLS])

        ids_in = sem("ids_in")
        idx_ready = sem("idx_ready")
        w0_in = sem("w0_in")
        w1_in = [sem("w1_in0"), sem("w1_in1")]
        w1_hi_ready = sem("w1_hi_ready")
        w1_lo_ready = sem("w1_lo_ready")
        w0_ready = sem("w0_ready")
        ident_zero = sem("ident_zero")
        ident_ready = sem("ident_ready")
        zeroed = sem("zeroed")
        looked_up = sem("looked_up")
        looked_up0 = sem("looked_up0")
        idx_staged = sem("idx_staged")
        raw_used = sem("raw_used")
        xp0_ready = sem("xp0_ready")
        ones_ready = sem("ones_ready")
        ext_ready = sem("ext_ready")
        extb_ready = sem("extb_ready")
        t_ready = sem("t_ready")
        a_ready = sem("a_ready")
        z_ready = sem("z_ready")
        z_used = sem("z_used")
        h0_hi_ready = sem("h0_hi_ready")
        h0_lo_ready = sem("h0_lo_ready")
        part_ready = sem("part_ready")
        part_used = sem("part_used")
        xs_ready = sem("xs_ready")
        y_ready = sem("y_ready")
        dve_half = sem("dve_half")
        act_quad = sem("act_quad")
        pool_add = sem("pool_add")
        fold = sem("fold")
        x_out = sem("x_out")
        h1_out = [sem(f"h1_out{d}") for d in range(DQ)]
        staged_w2 = sem("staged_w2")

        w1_view = w1.rearrange("(i j) n -> j i n", j=P)
        w2_view = w2.rearrange("(i j) n -> j i n", j=P)
        w0b_sb = bd[:].rearrange("p g c -> p (g c)")[:, 0:NT0 * N].rearrange("p (t n) -> p t n", n=N)
        CH = 16
        stage = [w2_sb[:, 0:CH, :], w2_sb[:, CH:2 * CH, :]]
        block = ctx.enter_context(nc.Block())

        @block.sync
        def _(sp):
            sp.dma_start(ids_sb[:].rearrange("p (b f) -> p b f", f=F), ids.rearrange("(b p) f -> p b f", p=P)).then_inc(ids_in, 16)
            sp.dma_start(base_sb[:], id_base).then_inc(ids_in, 16)
            sp.dma_start(w0[:], w0a).then_inc(w0_in, 16)
            sp.dma_start(w0b_sb, w0b).then_inc(w0_in, 16)
            for c in range(F // CH):
                if c >= 2:
                    sp.wait_ge(w1_lo_ready, c - 1)
                sp.dma_start(stage[c % 2], w1_view[:, c * CH:(c + 1) * CH, :]).then_inc(w1_in[c % 2], 16)
            sp.dma_start(keep["dense"][:], dense.rearrange("(b p) d -> p b d", p=P)).then_inc(tail_loaded, 16)
            sp.dma_start(keep["wt1"][:], wt1[0:3 * P, :].rearrange("(k p) f -> p k f", p=P)).then_inc(tail_loaded, 16)
            sp.dma_start(keep["wt1d"][:], wt1[3 * P:3 * P + D, :]).then_inc(tail_loaded, 16)
            sp.dma_start(keep["wt2"][:], wt2.rearrange("(k p) f -> p k f", p=P)).then_inc(tail_loaded, 16)
            with nc.allow_non_contiguous_dma(reason="a few hundred words"):
                sp.dma_start(keep["wt3"][:], wt3.rearrange("(k p) o -> p (k o)", p=P)).then_inc(tail_loaded, 16)
                sp.dma_start(keep["bt1"][:], bt1.rearrange("(k p) -> p k", p=P)).then_inc(tail_loaded, 16)
                sp.dma_start(keep["bt2"][:], bt2.rearrange("(k p) -> p k", p=P)).then_inc(tail_loaded, 16)
            sp.wait_ge(w1_lo_ready, F // CH)
            sp.dma_start(w2_sb[:], w2_view[:, 0:F // 2, :]).then_inc(tail_loaded, 16)
            sp.wait_ge(xp0_ready, 1)
            sp.wait_ge(ones_ready, 1)

            with sp.Fori(0, GROUPS, 1) as k:
                rows = bass.ds((k // DQ) * P, P)
                sp.wait_ge(raw_used, (k // DQ) * DQ)
                sp.dma_start(x_dram[rows, bass.ds((k % DQ) * (DQ * FX), DQ * FX)],
                             xp[:].rearrange("p a c -> p (a c)")[:, bass.ds(k * (DQ * FX), DQ * FX)]).then_inc(x_out, 16)
                for d in range(DQ):
                    sp.wait_ge(fold, k * (3 * DQ) + 3 * (d + 2))
                    sp.dma_start(h1_dram[rows, bass.ds((k % DQ) * (DQ * N) + d * N, N)], h1[:, d, :]).then_inc(h1_out[d], 16)
            sp.wait_ge(x_out, 16 * GROUPS)
            for d in range(DQ):
                sp.wait_ge(h1_out[d], 16 * GROUPS)

        def lookup(k_idx, out_ap, done):
            nc.gpsimd.indirect_dma_start(out=out_ap, out_offset=None, in_=tables,
                                         in_offset=bass.IndirectOffsetOnAxis(ap=k_idx, axis=0)).then_inc(done, 16)

        @block.gpsimd
        def _(pool):
            nc.gpsimd.memset(ident[:], 0.0).then_inc(ident_zero, 1)
            pool.wait_ge(ids_in, 32)
            for b in range(BLOCKS):
                ins = nc.gpsimd.tensor_tensor(idx[:, b * F:(b + 1) * F], ids_sb[:, b * F:(b + 1) * F], base_sb[:], ALU.add)
            ins.then_inc(idx_ready, 1)
            pool.wait_ge(idx_ready, 1)
            for f in range(F):
                lookup(idx[:, f:f + 1], raw0[:, f * D:(f + 1) * D], looked_up0)
                if f == 0:
                    pool.wait_ge(ident_zero, 1)
                    nc.gpsimd.affine_select(out=ident[:], in_=ident[:], compare_op=ALU.not_equal, fill=1.0, base=0,
                                            pattern=[[-1, P]], channel_multiplier=1).then_inc(ident_ready, 1)
            nc.gpsimd.tensor_copy(idx_now[:], idx[:, F:F + GATHERS]).then_inc(idx_staged, 1)
            pool.wait_ge(idx_staged, 1)
            for f in range(GATHERS):
                lookup(idx_now[:, f:f + 1], raw[:, f * D:(f + 1) * D], looked_up)

            def group(k, gather):
                pool.wait_ge(part_ready, k + 1)
                h0s = h0sum[:, bass.ds((k // DQ) * P, P)]
                nc.gpsimd.tensor_tensor(h0s, h0s, h0part[:], ALU.add).then_inc(part_used, 1)
                given = 0
                for d in range(DQ):
                    if gather and d == 1:
                        pool.wait_ge(raw_used, k + 1)
                        nc.gpsimd.tensor_copy(idx_now[:], idx[:, bass.ds(k * GATHERS + (F + GATHERS), GATHERS)]).then_inc(idx_staged, 1)
                        pool.wait_ge(idx_staged, k + 2)
                    for a in range(1, NA):
                        n = d * NA + a
                        pool.wait_ge(act_quad, act_done(k, n + 1))
                        if a > 1:
                            pool.wait_ge(pool_add, k * (DQ * ADDS) + (d * ADDS + a - 1))
                        acc = acc_p[:, d % 2, :]
                        nc.gpsimd.tensor_tensor(acc, acc, tmp[:, tmp_slot(d, a), :], ALU.add).then_inc(pool_add, 1)
                        done = (d - 1) * ADDS + a
                        while gather and given < GATHERS and given * (DQ - 1) * ADDS < done * GATHERS:
                            lookup(idx_now[:, given:given + 1], raw[:, given * D:(given + 1) * D], looked_up)
                            given += 1

            pool.wait_ge(zeroed, 1)
            with pool.Fori(0, GROUPS - DQ - 1, 1) as k:
                group(k, True)
            with pool.Fori(GROUPS - DQ - 1, GROUPS, 1) as k:
                group(k, False)

        def move_raw(m):
            where = xp[:, bass.ds((m // DQ) * D + D, D), bass.ds((m % DQ) * GATHERS, GATHERS)]
            nc.scalar.activation(where, raw[:].rearrange("p (f d) -> p d f", d=D), ACT.Copy).then_inc(raw_used, 1)

        @block.scalar
        def _(act):
            def rotated(g, a):
                act.wait_ge(t_ready, g * TT + (a + 1))
                act.wait_ge(z_ready, g * NT0)
                nc.scalar.activation(rota[:, a, :], tb[:, a % TBANKS, :], ACT.Copy).then_inc(a_ready, 1)

            def extend(g):
                act.wait_ge(raw_used, g // DQ * DQ)
                act.wait_ge(xs_ready, g * DQ)
                act.wait_ge(t_ready, g * TT)
                repeat(xp[:, bass.ds(g * DQ, DQ), 0:F])

            def repeat(src):
                nc.scalar.activation(ext[:, :, 0:F], src, ACT.Copy)
                nc.scalar.activation(ext[:, :, F:2 * F], src, ACT.Copy)
                nc.scalar.activation(ext[:, :, 2 * F:EXTW], src[:, :, 0:EXTW - 2 * F], ACT.Copy).then_inc(ext_ready, 1)

            def pair(g, kb):
                act.wait_ge(ext_ready, g + 1)
                row = ext[:, :, F - 1 - 2 * kb:]
                two = bass.AP(row.tensor, row.offset, [list(row.ap[0]), [EXTW, DQ], [1, 2], [1, F]])
                nc.scalar.activation(extb[:, kb, :, :].rearrange("p d (h i) -> p d h i", h=2), two, ACT.Copy).then_inc(extb_ready, 1)

            def high(g, part):
                cols = slice(0, 3 * P) if part == 0 else slice(3 * P, COLS)
                act.wait_ge(z_used, (g + 1) * NT0)
                nc.scalar.activation(h0_hi[:, cols], l0acc[:, cols], ACT.Copy).then_inc(h0_hi_ready, 1)

            for c in range(F // CH):
                act.wait_ge(w1_in[c % 2], 16 * (c // 2 + 1))
                nc.scalar.activation(w1_hi[:, c * CH * N:(c + 1) * CH * N], stage[c % 2].rearrange("p i n -> p (i n)"),
                                     ACT.Copy).then_inc(w1_hi_ready, 1)
            nc.scalar.sem_inc(act_quad, AHEAD_A)
            act.wait_ge(looked_up0, 16 * F)
            nc.scalar.activation(xp[:, 0:D, 0:F], raw0[:].rearrange("p (f d) -> p d f", d=D), ACT.Copy).then_inc(xp0_ready, 1)
            act.wait_ge(xp0_ready, 1)
            repeat(xp[:, 0:DQ, 0:F])
            for kb in range(ROTB):
                pair(0, kb)
            for a in range(ROTA):
                act.wait_ge(t_ready, a + 1)
                nc.scalar.activation(rota[:, a, :], tb[:, a % TBANKS, :], ACT.Copy).then_inc(a_ready, 1)
            high(0, 0)

            def group(k, gathered, layer0):
                for s in range(SLOTS):
                    d, q = s // QUADS, s % QUADS
                    if q in ACT_QUADS:
                        a = ACT_QUADS.index(q)
                        if a == 0:
                            act.wait_ge(xs_ready, k * DQ + (d + 1))
                            act.wait_ge(fold, k * (3 * DQ) + max(0, 3 * (d - 1) + 1))
                            out = acc_p[:, d % 2, :]
                        else:
                            act.wait_ge(pool_add, k * (DQ * ADDS) + max(0, d * ADDS + a - TMPS))
                            out = tmp[:, tmp_slot(d, a), :]
                        act.wait_ge(y_ready, k * SLOTS + (s + 1))
                        for m in range(QUAD):
                            i = q * QUAD + m
                            ins = nc.scalar.activation(out[:, m * N:(m + 1) * N], yq[:, s % YBANKS, m * N:(m + 1) * N],
                                                       ACT.Copy, scale=xs[:, d, i:i + 1])
                        ins.then_inc(act_quad, 1)
                    if gathered and s == 1:
                        act.wait_ge(looked_up, k * (16 * GATHERS) + 16 * GATHERS)
                        move_raw(k)
                    if s == HIGH_SLOT:
                        act.wait_ge(y_ready, k * SLOTS)
                        act.wait_ge(part_ready, k + 1)
                        high(k, 1)
                    if layer0:
                        if s == EXT_SLOT:
                            extend(k + 1)
                        for kb in range(ROTB):
                            if s == EXTB_SLOT[kb]:
                                pair(k + 1, kb)
                        for a in range(ROTA):
                            if s == T_SLOT[a] + 1:
                                rotated(k + 1, a)
                        if s == SLOTS - 1:
                            act.wait_ge(y_ready, k * SLOTS + 3 * QUADS)
                            high(k + 1, 0)

            with act.Fori(0, GROUPS - DQ, 1) as k:
                group(k, True, True)
            with act.Fori(GROUPS - DQ, GROUPS - 1, 1) as k:
                group(k, False, True)
            group(GROUPS - 1, False, False)

        @block.vector
        def _(dve):
            def product(g, n):
                kb, a = TILES0[n]
                dve.wait_ge(a_ready, g * ROTA + (a + 1))
                dve.wait_ge(t_ready, g * TT + (ROTA + kb + 1))
                dve.wait_ge(z_used, g * NT0 + max(0, n - ZBUFS + 1))
                nc.vector.tensor_tensor(z[:, n % ZBUFS, :], tb[:, (ROTA + kb) % TBANKS, :], rota[:, a, :],
                                        ALU.mult).then_inc(z_ready, 1)

            def low(g, part):
                cols = slice(0, 3 * P) if part == 0 else slice(3 * P, COLS)
                dve.wait_ge(h0_hi_ready, g * 2 + (part + 1))
                nc.vector.tensor_tensor(h0_lo[:, cols], l0acc[:, cols], h0_hi[:, cols].bitcast(F32),
                                        ALU.subtract).then_inc(h0_lo_ready, 1)

            def sum_depths(g):
                dve.wait_ge(part_used, g)
                nc.vector.tensor_reduce(h0part[:], l0acc[:].rearrange("p (d b) -> p b d", d=DQ), AX.X,
                                        ALU.add).then_inc(part_ready, 1)

            def scalars(g, d):
                nc.vector.tensor_copy(xs[:, d, :], ext[:, d, 0:F]).then_inc(xs_ready, 1)

            nc.vector.memset(xp[:, :, F:FX], 1.0).then_inc(ones_ready, 1)
            nc.vector.memset(h0sum[:], 0.0)
            nc.vector.memset(acc_d[:], 0.0)
            nc.vector.sem_inc(dve_half, 2 * AHEAD_D)
            nc.vector.memset(acc_p[:], 0.0).then_inc(zeroed, 1)
            dve.wait_ge(w0_in, 32)
            nc.vector.tensor_tensor(w0[0:F, 0, :], w0[0:F, 0, :], w0b_sb[0:F, 0, :], ALU.add)
            nc.vector.tensor_tensor(w0[F:P, NT0 - 1, :], w0[F:P, NT0 - 1, :], w0b_sb[F:P, NT0 - 1, :], ALU.add)
            nc.vector.tensor_tensor(w0[:, 1:ROTA - 1, :], w0[:, 1:ROTA - 1, :], w0b_sb[:, 1:ROTA - 1, :], ALU.add)
            nc.vector.tensor_tensor(w0[:, ROTA:NT0 - 1, :], w0[:, ROTA:NT0 - 1, :], w0b_sb[:, ROTA:NT0 - 1, :],
                                    ALU.add).then_inc(w0_ready, 1)
            dve.wait_ge(w0_ready, 1)
            nc.vector.memset(bd[:], 0.0)
            for c in range(F // CH):
                cols = slice(c * CH * N, (c + 1) * CH * N)
                dve.wait_ge(w1_hi_ready, c + 1)
                nc.vector.tensor_tensor(w1_lo[:, cols], stage[c % 2].rearrange("p i n -> p (i n)"), w1_hi[:, cols].bitcast(F32),
                                        ALU.subtract).then_inc(w1_lo_ready, 1)
            dve.wait_ge(ext_ready, 1)
            for d in range(DQ - 1):
                scalars(0, d)
            for n in range(NT0):
                product(0, n)
            low(0, 0)
            sum_depths(0)

            def fold_step(k, d, step):
                before = k * (3 * DQ) + 3 * d
                par, acc = (d + 1) % 2, acc_d[:, (d + 1) % 2, :]
                if step == 0:
                    dve.wait_ge(pool_add, k * (DQ * ADDS) + d * ADDS)
                    dve.wait_ge(dve_half, halves_done(k, d * ND))
                    nc.vector.tensor_tensor(acc, acc, acc_p[:, par, :], ALU.add).then_inc(fold, 1)
                elif step == 1:
                    dve.wait_ge(fold, before + 1)
                    nc.vector.tensor_tensor(acc[:, 0:2 * N], acc[:, 0:2 * N], acc[:, 2 * N:4 * N], ALU.add).then_inc(fold, 1)
                else:
                    dve.wait_ge(fold, before + 2)
                    slot = (d - 1) % DQ
                    if d:
                        dve.wait_ge(h1_out[slot], 16 * k)
                    if d == DQ - 1:
                        dve.wait_ge(h1_out[d], 16 * k)
                    nc.vector.tensor_tensor(h1[:, slot, :], acc[:, 0:N], acc[:, N:2 * N], ALU.add).then_inc(fold, 1)

            def group(k, layer0):
                dve.wait_ge(act_quad, act_done(k, 0))
                dve.wait_ge(dve_half, halves_done(k, 0))
                scalars(k, DQ - 1)
                for s in range(SLOTS):
                    d, q = s // QUADS, s % QUADS
                    if q in DVE_QUADS:
                        j = DVE_QUADS.index(q)
                        dve.wait_ge(y_ready, k * SLOTS + (s + 1))
                        if j == 0:
                            dve.wait_ge(xs_ready, k * DQ + (d + 1))
                            dve.wait_ge(fold, k * (3 * DQ) + 3 * d)
                        for m in range(QUAD):
                            i = q * QUAD + m
                            part, out = yq[:, s % YBANKS, m * N:(m + 1) * N], acc_d[:, d % 2, m * N:(m + 1) * N]
                            if j == 0:
                                ins = nc.vector.tensor_scalar(out, part, xs[:, d, i:i + 1], None, ALU.mult)
                            else:
                                if m % 2 == 0:
                                    dve.wait_ge(dve_half, halves_done(k, d * ND + j - 1) + (m // 2 + 1))
                                ins = nc.vector.scalar_tensor_tensor(out=out, in0=part, scalar=xs[:, d, i:i + 1], in1=out,
                                                                     op0=ALU.mult, op1=ALU.add)
                            if m % 2 == 1:
                                ins.then_inc(dve_half, 1)
                    if s == LOW_SLOT:
                        low(k, 1)
                    if q in FOLD_AFTER:
                        fold_step(k, d, FOLD_AFTER[q])
                    if layer0:
                        for n in range(NT0):
                            if s == Z_SLOT[n]:
                                product(k + 1, n)
                        if d == DQ - 1 and q in COPY_SLOT:
                            c = COPY_SLOT[q]
                            dve.wait_ge(act_quad, act_done(k, (c + 1) * NA))
                            dve.wait_ge(dve_half, halves_done(k, (c + 1) * ND))
                            dve.wait_ge(ext_ready, k + 2)
                            scalars(k + 1, c)
                        if s == SLOTS - 1:
                            low(k + 1, 0)
                            sum_depths(k + 1)

            with dve.Fori(0, GROUPS - 1, 1) as k:
                group(k, True)
            group(GROUPS - 1, False)
            for step in range(3):
                fold_step(GROUPS, 0, step)

        @block.tensor
        def _(pe):
            def transposes(g, j):
                if j < ROTA:
                    pe.wait_ge(ext_ready, g + 1)
                    rows = ext[:, :, 8 * j:8 * j + P]
                else:
                    pe.wait_ge(extb_ready, g * ROTB + (j - ROTA + 1))
                    rows = extb[:, j - ROTA, :, :]
                if j < TBANKS:
                    pe.wait_ge(z_ready, g * NT0)
                elif j - TBANKS < ROTA:
                    pe.wait_ge(a_ready, g * ROTA + (j - TBANKS + 1))
                else:
                    pe.wait_ge(z_ready, g * NT0 + (LAST_OF_KB[j - TBANKS - ROTA] + 1))
                for d in range(DQ):
                    ins = nc.tensor.transpose(tb[:, j % TBANKS, d * P:(d + 1) * P], rows[:, d, :], ident[:])
                ins.then_inc(t_ready, 1)

            def contract0(g, n):
                pe.wait_ge(z_ready, g * NT0 + (n + 1))
                if n == 0:
                    pe.wait_ge(h0_lo_ready, g * 2)
                    pe.wait_ge(part_ready, g)
                nc.tensor.matmul(l0acc[:], w0[:, n, :], z[:, n % ZBUFS, :], start=(n == 0), stop=(n == NT0 - 1)).then_inc(z_used, 1)

            pe.wait_ge(ident_ready, 1)
            for j in range(ROTA + 1):
                transposes(0, j)
            pe.wait_ge(w0_ready, 1)
            for n in range(NT0):
                if n in LAST_OF_KB[:-1]:
                    transposes(0, ROTA + TILES0[n][0] + 1)
                contract0(0, n)
            pe.wait_ge(w1_lo_ready, F // CH)

            def group(k, layer0):
                for s in range(SLOTS):
                    d, q = s // QUADS, s % QUADS
                    if q == 0:
                        pe.wait_ge(h0_lo_ready, k * 2 + (1 if d < DQ - 1 else 2))
                    before = s - YBANKS
                    if before % QUADS in DVE_QUADS:
                        pe.wait_ge(dve_half, halves_done(k, quads_before(DVE_QUADS, before + 1)))
                    else:
                        pe.wait_ge(act_quad, act_done(k, quads_before(ACT_QUADS, before + 1)))
                    lhs = slice(d * P, (d + 1) * P)
                    rhs = slice(q * QUAD * N, (q + 1) * QUAD * N)
                    bank = yq[:, s % YBANKS, :]
                    nc.tensor.matmul(bank, h0_hi[:, lhs], w1_hi[:, rhs], start=True, stop=False)
                    nc.tensor.matmul(bank, h0_hi[:, lhs], w1_lo[:, rhs], start=False, stop=False)
                    nc.tensor.matmul(bank, h0_lo[:, lhs], w1_hi[:, rhs], start=False, stop=True).then_inc(y_ready, 1)
                    if layer0:
                        for j in range(TT):
                            if s == T_SLOT[j]:
                                transposes(k + 1, j)
                        for n in range(NT0):
                            if s == L0_SLOT[n]:
                                contract0(k + 1, n)

            with pe.Fori(0, GROUPS - 1, 1) as k:
                group(k, True)
            group(GROUPS - 1, False)


def layer_2_and_mlp(nc, keep, tail_loaded, x_dram, h1_dram, w2, y):
    with ExitStack() as ctx:
        def sb(name, shape, dt=F32):
            return ctx.enter_context(nc.sbuf_tensor(name, shape, dt))

        def sem(name):
            return ctx.enter_context(nc.semaphore(name))

        GB = P // 8
        W = 4 * FX
        SETS = 3
        w2_sb = [keep["w2"], sb("w2_rest", [P, F // 2, N])]
        bd = [keep["bd"], sb("bd_odd", [P, GB, W])]
        stack = [keep["stack"], sb("stack_odd", [P, GB, N])]
        gs = sb("gs", [P, FX, HALF])
        h1sum = sb("h1sum", [P, B])
        h2sum = sb("h2sum", [P, B])
        dense_t = sb("dense_t", [D, B])
        hid1 = sb("hid1", [P, 4, B])
        hid2 = sb("hid2", [P, 2, B])
        y_sb = sb("y_sb", [1, B])
        ps = ctx.enter_context(nc.psum_tensor("ps", [P, 8, 512], F32))

        w2_in = sem("w2_in")
        bd_in = [sem("bd_in_even"), sem("bd_in_odd")]
        stack_in = [sem("stack_in_even"), sem("stack_in_odd")]
        bd_zeroed = sem("bd_zeroed")
        g_ready = sem("g_ready")
        g_act = sem("g_act")
        g_dve = sem("g_dve")
        w2_done = sem("w2_done")
        sum_ready = sem("sum_ready")
        dense_turned = sem("dense_turned")
        dense_ready = sem("dense_ready")
        lin1 = sem("lin1")
        hid1_ready = sem("hid1_ready")
        lin2 = sem("lin2")
        hid2_ready = sem("hid2_ready")
        lin3 = sem("lin3")
        y_ready3 = sem("y_in_sbuf")
        y_out = sem("y_out")

        h1_view = h1_dram.rearrange("(q g s) (d n) -> q (s d) g n", s=8, g=GB, n=N)
        x_view = x_dram.rearrange("(q g s) (d f) -> q s d g f", s=8, g=GB, f=FX)
        block = ctx.enter_context(nc.Block())

        def load_bd(eng, q, samples):
            for s in samples:
                eng.dma_start(bd[q % 2][D * s:D * (s + 1), :, (s % 4) * FX:(s % 4 + 1) * FX], x_view[q, s]).then_inc(bd_in[q % 2], 16)

        @block.sync
        def _(sp):
            for q in range(BLOCKS):
                if q == 1:
                    sp.wait_ge(bd_zeroed, 1)
                if q >= 2:
                    sp.wait_ge(g_ready, (q - 1) * GB)
                sp.dma_start(stack[q % 2][:], h1_view[q]).then_inc(stack_in[q % 2], 16)
                load_bd(sp, q, range(4))
            sp.wait_ge(y_ready3, 1)
            sp.dma_start(y.rearrange("b o -> o b"), y_sb[:]).then_inc(y_out, 16)
            sp.wait_ge(y_out, 16)

        @block.gpsimd
        def _(pool):
            nc.gpsimd.memset(bd[1][:], 0.0).then_inc(bd_zeroed, 1)

        def take_g(eng, copy, t, done):
            half, h = t // (2 * GB), t % (2 * GB)
            eng.wait_ge(g_ready, t + 1)
            if half:
                eng.wait_ge(w2_done, half)
                eng.wait_ge(sum_ready, 2 * half - 1)
            src = ps[:, 2 * (t % SETS):2 * (t % SETS) + 2, 0:W].rearrange("p r (s i) -> p r s i", i=FX)
            dst = gs[:, :, 8 * h:8 * h + 8].rearrange("p i (r s) -> p r s i", s=4)
            copy(dst, src).then_inc(done, 1)

        @block.scalar
        def _(act):
            act.dma_start(w2_sb[1][:], w2.rearrange("(i j) n -> j i n", j=P)[:, F // 2:F, :]).then_inc(w2_in, 16)
            for q in range(2):
                if q == 1:
                    act.wait_ge(bd_zeroed, 1)
                load_bd(act, q, range(4, 8))
            act.wait_ge(dense_turned, 1)
            nc.scalar.activation(dense_t[:], ps[0:D, 7, :], ACT.Copy).then_inc(dense_ready, 1)
            for t in range(0, BLOCKS * GB, 2):
                if t == GB or t == 2 * GB:
                    q = t // GB + 1
                    act.wait_ge(g_ready, t)
                    load_bd(act, q, range(4, 8))
                take_g(act, lambda o, i: nc.scalar.activation(o, i, ACT.Copy), t, g_act)
            for m in range(4):
                act.wait_ge(lin1, m + 1)
                nc.scalar.activation(hid1[:, m, :], ps[:, m, :], ACT.Relu, bias=keep["bt1"][:, m:m + 1]).then_inc(hid1_ready, 1)
            for m in range(2):
                act.wait_ge(lin2, m + 1)
                nc.scalar.activation(hid2[:, m, :], ps[:, 4 + m, :], ACT.Relu, bias=keep["bt2"][:, m:m + 1]).then_inc(hid2_ready, 1)

        @block.vector
        def _(dve):
            for t in range(1, BLOCKS * GB, 2):
                take_g(dve, lambda o, i: nc.vector.tensor_copy(o, i), t, g_dve)
                half, h = t // (2 * GB), t % (2 * GB)
                if h == 2 * GB - 1:
                    cols = slice(half * HALF, (half + 1) * HALF)
                    dve.wait_ge(g_act, (half + 1) * GB)
                    dve.wait_ge(g_dve, (half + 1) * GB)
                    nc.vector.tensor_copy(h1sum[:, cols], gs[:, F, :]).then_inc(sum_ready, 1)
                    dve.wait_ge(w2_done, half + 1)
                    nc.vector.tensor_copy(h2sum[:, cols], ps[:, 6 + half, 0:HALF]).then_inc(sum_ready, 1)
            dve.wait_ge(lin3, 1)
            nc.vector.tensor_copy(y_sb[:], ps[0:1, 7, :]).then_inc(y_ready3, 1)

        @block.tensor
        def _(pe):
            pe.wait_ge(tail_loaded, 16 * 8)
            for q in range(BLOCKS):
                ins = nc.tensor.transpose(ps[0:D, 7, q * P:(q + 1) * P], keep["dense"][:, q, :], keep["ident"][:])
            ins.then_inc(dense_turned, 1)
            for half in range(2):
                for q in (2 * half, 2 * half + 1):
                    pe.wait_ge(stack_in[q % 2], 16 * (q // 2 + 1))
                    pe.wait_ge(bd_in[q % 2], 8 * 16 * (q // 2 + 1))
                    for g in range(GB):
                        t = q * GB + g
                        if t >= SETS:
                            pe.wait_ge(g_dve if (t - SETS) % 2 else g_act, (t - SETS) // 2 + 1)
                        for r in range(2):
                            ins = nc.tensor.matmul(ps[:, 2 * (t % SETS) + r, 0:W], stack[q % 2][64 * r:64 * r + 64, g, :],
                                                   bd[q % 2][64 * r:64 * r + 64, g, :], start=True, stop=True)
                        ins.then_inc(g_ready, 1)
                pe.wait_ge(g_act, (half + 1) * GB)
                pe.wait_ge(g_dve, (half + 1) * GB)
                pe.wait_ge(w2_in, 16)
                if half == 1:
                    pe.wait_ge(dense_ready, 1)
                for i in range(F):
                    ins = nc.tensor.matmul(ps[:, 6 + half, 0:HALF], w2_sb[i // (F // 2)][:, i % (F // 2), :], gs[:, i, :],
                                           start=(i == 0), stop=(i == F - 1))
                ins.then_inc(w2_done, 1)
            pe.wait_ge(dense_ready, 1)
            pe.wait_ge(sum_ready, 4)
            for m in range(4):
                cols = slice(m * P, (m + 1) * P)
                for n, (w, x) in enumerate([(keep["wt1d"][:, cols], dense_t[:]), (keep["wt1"][:, 0, cols], keep["h0sum"][:]),
                                            (keep["wt1"][:, 1, cols], h1sum[:]), (keep["wt1"][:, 2, cols], h2sum[:])]):
                    ins = nc.tensor.matmul(ps[:, m, :], w, x, start=(n == 0), stop=(n == 3))
                ins.then_inc(lin1, 1)
            for m in range(2):
                for n in range(4):
                    pe.wait_ge(hid1_ready, n + 1)
                    ins = nc.tensor.matmul(ps[:, 4 + m, :], keep["wt2"][:, n, m * P:(m + 1) * P], hid1[:, n, :],
                                           start=(n == 0), stop=(n == 3))
                ins.then_inc(lin2, 1)
            for m in range(2):
                pe.wait_ge(hid2_ready, m + 1)
                ins = nc.tensor.matmul(ps[0:1, 7, :], keep["wt3"][:, m:m + 1], hid2[:, m, :], start=(m == 0), stop=(m == 1))
            ins.then_inc(lin3, 1)


def kernel(**inputs):
    import concourse.bacc as _bacc
    from concourse.bass_utils import run_bass_kernel_spmd as _run

    a = {name: np.ascontiguousarray(x) for name, x in inputs.items()}
    tables = np.concatenate([a[f"tbl_{f}"] for f in range(F)], axis=0)
    sizes = [a[f"tbl_{f}"].shape[0] for f in range(F)]
    id_base = np.ascontiguousarray(np.broadcast_to(np.array([sum(sizes[:f]) for f in range(F)], np.int32), (P, F)))
    part = np.arange(P)
    first = np.stack([(part + 8 * r) % F for _, r in TILES0], 1)
    second = np.stack([(part - (2 * kb + (part < F))) % F for kb, _ in TILES0], 1)
    w0 = a["L0_rec_W0"]
    arrays = {
        "tables": tables, "ids": a["ids"], "id_base": id_base, "w0a": w0[first * F + second], "w0b": w0[second * F + first],
        "w1": a["L0_rec_W1"], "w2_in": a["L0_rec_W2"], "dense": a["dense_ctx"], "wt1_in": a["W_top1"], "bt1_in": a["b_top1"],
        "wt2_in": a["W_top2"], "bt2_in": a["b_top2"], "wt3_in": a["W_top3"],
    }
    nc = _bacc.Bacc("TRN2", target_bir_lowering=False, num_devices=1)
    args = [nc.dram_tensor(f"{n}_dram", x.shape, mybir.dt.from_np(x.dtype), kind="ExternalInput").ap() for n, x in arrays.items()]
    args.append(nc.dram_tensor("y_dram", (B, 1), F32, kind="ExternalOutput").ap())
    dlrm(nc, *args)
    r = _run(nc, [{f"{n}_dram": x for n, x in arrays.items()}], core_ids=[0])
    return r.results[0]["y_dram"]
```

```python
from contextlib import ExitStack

import numpy as np

import concourse.bass as bass
from concourse import mybir

ALU = mybir.AluOpType
ACT = mybir.ActivationFunctionType
AX = mybir.AxisListType
F32 = mybir.dt.float32
F32R = mybir.dt.float32r
I32 = mybir.dt.int32

P = 128
B = 512
F = 64
D = 16
N = 128
COLS = 512
SAMPLES = COLS // D
GROUPS = B // SAMPLES
TILES = COLS // P
TS = P // D
BLOCK = 4
BLOCKS = GROUPS // BLOCK

QUAD = 4
QUADS = F // QUAD
SLOTS = TILES * QUADS
YBANKS = 4

ROTA = 5
ROTB = 4
TILES0 = [(kb, a) for kb in range(ROTB) for a in range(ROTA if kb == 0 else ROTA - 1)]
NT0 = len(TILES0)
ZBUFS = 3

DVE_QUADS = [q for q in range(QUADS) if q % 2 == 0]
ACT_QUADS = [q for q in range(QUADS) if q % 2 == 1]
ND, NA = len(DVE_QUADS), len(ACT_QUADS)
ADDS = NA - 1
TMPS = 3
FOLD_AFTER = {DVE_QUADS[1]: 0, DVE_QUADS[3]: 1, DVE_QUADS[4]: 2}

HIGH_SLOT = 5
LOW_SLOT = 10
XS3_SLOT = 4
XT_SLOT = 8
X_OUT_SLOT = 9
L0_SLOT = [14 + (n * 44) // (NT0 - 1) for n in range(NT0)]
Z_SLOT = [s - 4 for s in L0_SLOT]
COPY_SLOT = {2: 0, 3: 1, 4: 2}
HIGH0_SLOT = 59
LOW0_SLOT = 60
SUM_SLOT = 12
G_SLOT = 13
G_OUT_SLOT = 15
H_SLOT = 18
H_OUT_SLOT = 19
GX_USES = 2 + TILES
LEAD = 1
GX_END = GROUPS * GX_USES + BLOCKS - 1 + LEAD


def quads_before(quads, slot):
    return slot // QUADS * len(quads) + sum(q < slot % QUADS for q in quads)


AHEAD_D = LEAD - quads_before(DVE_QUADS, 1 - YBANKS)
AHEAD_A = LEAD - quads_before(ACT_QUADS, 1 - YBANKS)


def halves_done(k, quads):
    return k * (2 * TILES * ND) + 2 * (quads + AHEAD_D)


def act_done(k, quads):
    return k * (TILES * NA) + (quads + AHEAD_A)


def adds_done(k, adds):
    return k * (TILES * ADDS) + (adds + LEAD)


def folds_done(k, folds):
    return k * (3 * TILES) + (folds + LEAD)


def gx_count(k, block, uses):
    return k * GX_USES + block + (uses + LEAD)


def tmp_slot(t, a):
    return (t * ADDS + a - 1) % TMPS


def in_loops(eng, group, phase):
    with eng.Fori(0, BLOCKS - 1, 1) as block:
        with eng.Fori(0, BLOCK, 1) as q:
            group(eng.snap(block * BLOCK + q), q, block, True)
        phase(block)
    last = BLOCKS - 1
    with eng.Fori(0, BLOCK - 1, 1) as q:
        group(eng.snap(q + last * BLOCK), q, last, True)
    group(GROUPS - 1, BLOCK - 1, last, False)
    phase(last)


def dlrm(nc, tables, ids, id_base, mask, eye, w0a, w0b, w1, w2, dense, wt1, bt1, wt2, bt2, wt3, y):
    with ExitStack() as ctx:
        def sb(name, shape, dt=F32):
            return ctx.enter_context(nc.sbuf_tensor(name, shape, dt))

        keep = {
            "h0sum": sb("h0sum", [P, B]), "h1sum": sb("h1sum", [P, SAMPLES + B]), "h2sum": sb("h2sum", [P, TS + B]),
            "ident": sb("ident", [P, P]),
        }
        cin(nc, keep, tables, ids, id_base, mask, eye, w0a, w0b, w1, w2)
        mlp(nc, keep, dense, wt1, bt1, wt2, bt2, wt3, y)


def cin(nc, keep, tables, ids, id_base, mask, eye, w0a, w0b, w1, w2):
    x_dram = nc.dram_tensor("x_scratch", (GROUPS, F, COLS), F32, kind="Internal").ap()
    with ExitStack() as ctx:
        def sb(name, shape, dt=F32):
            return ctx.enter_context(nc.sbuf_tensor(name, shape, dt))

        def psum(name, shape):
            return ctx.enter_context(nc.psum_tensor(name, shape, F32))

        def sem(name):
            return ctx.enter_context(nc.semaphore(name))

        h0sum, h1sum, h2sum, ident = keep["h0sum"], keep["h1sum"], keep["h2sum"], keep["ident"]
        w1_hi = sb("w1_hi", [P, F * N], F32R)
        w1_lo = sb("w1_lo", [P, F * N], F32R)
        w2_sb = sb("w2_sb", [P, F, N])
        w0 = sb("w0", [P, NT0, N])
        gbuf = sb("gbuf", [P, F, P])
        ids_sb = sb("ids_sb", [P, GROUPS * D], I32)
        base_sb = sb("base_sb", [P, D], I32)
        idx = sb("idx", [P, (GROUPS + 1) * D], I32)
        idx_now = sb("idx_now", [P, D], I32)
        raw = sb("raw", [P, D * D])
        rota = sb("rota", [P, ROTA, COLS])
        rotb = sb("rotb", [P, ROTB, COLS])
        xnext = sb("xnext", [P, TILES, F])
        xs = sb("xs", [P, TILES, F])
        mask_sb = sb("mask_sb", [P, TS])
        bd = sb("bd", [P, 2, TS, F])
        z = sb("z", [P, ZBUFS, COLS])
        h0_hi = sb("h0_hi", [P, COLS], F32R)
        h0_lo = sb("h0_lo", [P, COLS], F32R)
        tmp = sb("tmp", [P, TMPS, QUAD * N])
        acc_d = sb("acc_d", [P, 2, QUAD * N])
        acc_p = sb("acc_p", [P, 2, QUAD * N])
        h1 = sb("h1", [P, TILES, N])

        yq = psum("yq", [P, YBANKS, QUAD * N])
        l0acc = psum("l0acc", [P, COLS])
        gx = psum("gx", [P, COLS])

        ids_in = sem("ids_in")
        idx_ready = sem("idx_ready")
        consts_in = sem("consts_in")
        w0_in = sem("w0_in")
        w0_ready = sem("w0_ready")
        w1_in = [sem("w1_in0"), sem("w1_in1")]
        w1_hi_ready = sem("w1_hi_ready")
        w1_lo_ready = sem("w1_lo_ready")
        w2_in = sem("w2_in")
        looked_up = sem("looked_up")
        idx_staged = sem("idx_staged")
        x_written = sem("x_written")
        xt_in = sem("xt_in")
        rotb_in = [sem(f"rotb_in{kb}") for kb in range(ROTB)]
        rota_in = [None] + [sem(f"rota_in{a}") for a in range(1, ROTA)]
        z_ready = sem("z_ready")
        z_used = sem("z_used")
        h0_hi_ready = sem("h0_hi_ready")
        h0_lo_ready = sem("h0_lo_ready")
        h0_summed = sem("h0_summed")
        xs_ready = sem("xs_ready")
        bd_ready = sem("bd_ready")
        y_ready = sem("y_ready")
        dve_half = sem("dve_half")
        act_quad = sem("act_quad")
        pool_add = sem("pool_add")
        fold = sem("fold")
        gx_ready = sem("gx_ready")
        gx_taken = sem("gx_taken")
        zeroed = sem("zeroed")
        first_x_out = sem("first_x_out")
        bd_zeroed = sem("bd_zeroed")

        w1_view = w1.rearrange("(i j) n -> j i n", j=P)
        w2_view = w2.rearrange("(i j) n -> j i n", j=P)
        w0b_sb = gbuf[:].rearrange("p i b -> p (i b)")[:, 0:NT0 * N].rearrange("p (t n) -> p t n", n=N)
        CH = F // 4
        stage = [w2_sb[:, 0:CH, :], w2_sb[:, CH:2 * CH, :]]
        block = ctx.enter_context(nc.Block())

        @block.sync
        def _(sp):
            for r in range(TILES):
                rows = slice(r * SAMPLES, (r + 1) * SAMPLES)
                sp.dma_start(ids_sb[rows, :].rearrange("s (g f) -> s g f", f=D),
                             ids[:, r * D:(r + 1) * D].rearrange("(g s) f -> s g f", s=SAMPLES)).then_inc(ids_in, 16)
            sp.dma_start(base_sb[:], id_base).then_inc(ids_in, 16)
            sp.dma_start(ident[:], eye).then_inc(consts_in, 16)
            sp.dma_start(mask_sb[:], mask).then_inc(consts_in, 16)
            sp.dma_start(w0[:], w0a).then_inc(w0_in, 16)
            sp.dma_start(w0b_sb, w0b).then_inc(w0_in, 16)
            for c in range(2):
                sp.dma_start(stage[c], w1_view[:, c * CH:(c + 1) * CH, :]).then_inc(w1_in[c], 16)

            def bring(g, z_done):
                sp.wait_ge(looked_up, g * (16 * D) + 16 * D)
                dst = x_dram[bass.ds(g, 1), :, :].rearrange("o (r f) (s d) -> (o r) s f d", f=D, d=D)
                for r in range(TILES):
                    sp.dma_start(dst[r], raw[r * SAMPLES:(r + 1) * SAMPLES, :].rearrange("s (f d) -> s f d", d=D)).then_inc(x_written, 16)
                sp.wait_ge(x_written, g * (16 * TILES) + 16 * TILES)
                if z_done is not None:
                    sp.wait_ge(z_ready, z_done)
                for h in range(2):
                    sp.dma_start(rota[h * F:(h + 1) * F, 0, :], x_dram[bass.ds(g, 1), :, :].rearrange("o f c -> (o f) c")).then_inc(xt_in, 16)
                sp.wait_ge(xt_in, g * 32 + 32)
                for kb in range(ROTB):
                    for h in range(2):
                        first = F - 2 * kb - (1 - h)
                        sp.dma_start(rotb[h * F:(h + 1) * F, kb, :], rota[first:first + F, 0, :]).then_inc(rotb_in[kb], 16)
                    for a in range(1, ROTA) if kb == 0 else ():
                        for h in range(2):
                            sp.dma_start(rota[h * F:(h + 1) * F, a, :], rota[8 * a:8 * a + F, 0, :]).then_inc(rota_in[a], 16)

            bring(0, None)
            bring(1, NT0 + LEAD)
            sp.wait_ge(w1_lo_ready, F // CH)
            sp.dma_start(w2_sb[:], w2_view).then_inc(w2_in, 16)
            with sp.Fori(1, GROUPS - 1, 1) as k:
                bring(k + 1, k * NT0 + (NT0 + LEAD))

        def lookups(first, last):
            for f in range(first, last):
                nc.gpsimd.indirect_dma_start(out=raw[:, f * D:(f + 1) * D], out_offset=None, in_=tables,
                                             in_offset=bass.IndirectOffsetOnAxis(ap=idx_now[:, f:f + 1], axis=0)).then_inc(looked_up, 16)

        @block.gpsimd
        def _(pool):
            def stage_idx(g):
                nc.gpsimd.tensor_copy(idx_now[:], idx[:, bass.ds(g * D, D)]).then_inc(idx_staged, 1)
                pool.wait_ge(idx_staged, g + 1)

            for s in (pool_add, bd_ready):
                nc.gpsimd.sem_inc(s, LEAD)
            nc.gpsimd.memset(idx[:, GROUPS * D:], 0)
            pool.wait_ge(ids_in, 16 * (TILES + 1))
            for g in range(GROUPS):
                ins = nc.gpsimd.tensor_tensor(idx[:, g * D:(g + 1) * D], ids_sb[:, g * D:(g + 1) * D], base_sb[:], ALU.add)
            ins.then_inc(idx_ready, 1)
            pool.wait_ge(idx_ready, 1)
            stage_idx(0)
            lookups(0, D)
            nc.gpsimd.memset(bd[:], 0.0).then_inc(bd_zeroed, 1)
            pool.wait_ge(x_written, 16 * TILES)
            stage_idx(1)
            lookups(0, D)
            pool.wait_ge(bd_zeroed, 1)
            pool.wait_ge(zeroed, 3)
            pool.wait_ge(consts_in, 32)

            def group(k, q, block_, layer0):
                given = 0
                for t in range(TILES):
                    if layer0 and t == 0:
                        pool.wait_ge(x_written, k * (16 * TILES) + 2 * 16 * TILES)
                        stage_idx(k + 2)
                    for a in range(1, NA):
                        pool.wait_ge(act_quad, act_done(k, t * NA + a + 1))
                        if a > 1:
                            pool.wait_ge(pool_add, adds_done(k, t * ADDS + a - 1))
                        acc = acc_p[:, t % 2, :]
                        nc.gpsimd.tensor_tensor(acc, acc, tmp[:, tmp_slot(t, a), :], ALU.add).then_inc(pool_add, 1)
                        if a == 1:
                            pool.wait_ge(xs_ready, k * TILES + (t + 1 + LEAD))
                            pool.wait_ge(gx_ready, gx_count(k, block_, ([0, 2, 4, 5] if layer0 else [0, 1, 3, 4])[t]))
                            out = bd[:, t % 2, :, :]
                            nc.gpsimd.tensor_tensor(out, xs[:, t:t + 1, :].to_broadcast([P, TS, F]),
                                                    mask_sb[:].unsqueeze(2).to_broadcast([P, TS, F]), ALU.mult).then_inc(bd_ready, 1)
                        upto = min(D, -(-(t * ADDS + a) * D // ((TILES - 1) * ADDS)))
                        if layer0 and upto > given:
                            lookups(given, upto)
                            given = upto

            in_loops(pool, group, lambda block_: None)
            pool.wait_ge(looked_up, (GROUPS + 1) * 16 * D)

        @block.scalar
        def _(act):
            def copy(out, in_, done):
                nc.scalar.activation(out, in_, ACT.Copy).then_inc(done, 1)

            def high(g, part):
                cols = slice(0, 3 * P) if part == 0 else slice(3 * P, COLS)
                copy(h0_hi[:, cols], l0acc[:, cols], h0_hi_ready)

            def x_out(g, uses):
                act.wait_ge(gx_ready, uses)
                act.wait_ge(xs_ready, g * TILES + LEAD)
                copy(xnext[:], gx[:].rearrange("p (t h i) -> p t h i", h=2, i=F)[:, :, 0, :], gx_taken)

            for s in (gx_taken, h0_hi_ready):
                nc.scalar.sem_inc(s, LEAD)
            nc.scalar.sem_inc(act_quad, AHEAD_A)
            for c in range(2):
                act.wait_ge(w1_in[c], 16)
                copy(w1_hi[:, c * CH * N:(c + 1) * CH * N], stage[c].rearrange("p i n -> p (i n)"), w1_hi_ready)
            for c in range(2, F // CH):
                act.wait_ge(w1_lo_ready, c - 1)
                act.dma_start(stage[c % 2], w1_view[:, c * CH:(c + 1) * CH, :]).then_inc(w1_in[c % 2], 16)
            for c in range(2, F // CH):
                act.wait_ge(w1_in[c % 2], 32)
                copy(w1_hi[:, c * CH * N:(c + 1) * CH * N], stage[c % 2].rearrange("p i n -> p (i n)"), w1_hi_ready)
            act.wait_ge(gx_ready, 1)
            copy(xnext[:], gx[:].rearrange("p (t h i) -> p t h i", h=2, i=F)[:, :, 0, :], first_x_out)
            act.wait_ge(z_used, NT0)
            high(0, 0)

            def group(k, q, block_, layer0):
                uses = 0
                for s in range(SLOTS):
                    t, qd = s // QUADS, s % QUADS
                    if qd in ACT_QUADS:
                        a = ACT_QUADS.index(qd)
                        if a == 0:
                            act.wait_ge(xs_ready, k * TILES + (t + 1 + LEAD))
                            act.wait_ge(fold, folds_done(k, max(0, 3 * (t - 1) + 1)))
                            out = acc_p[:, t % 2, :]
                        else:
                            act.wait_ge(pool_add, adds_done(k, max(0, t * ADDS + a - TMPS)))
                            out = tmp[:, tmp_slot(t, a), :]
                        act.wait_ge(y_ready, k * SLOTS + (s + 1))
                        for m in range(QUAD):
                            i = qd * QUAD + m
                            ins = nc.scalar.activation(out[:, m * N:(m + 1) * N], yq[:, s % YBANKS, m * N:(m + 1) * N],
                                                       ACT.Copy, scale=xs[:, t, i:i + 1])
                        ins.then_inc(act_quad, 1)
                    if s == HIGH_SLOT:
                        act.wait_ge(h0_lo_ready, k * 2 + (1 + LEAD))
                        high(k, 1)
                    if layer0 and s == X_OUT_SLOT:
                        x_out(k + 1, gx_count(k, block_, 1))
                        uses += 1
                    if qd == G_OUT_SLOT:
                        uses += 1
                        act.wait_ge(gx_ready, gx_count(k, block_, uses))
                        copy(gbuf[:, :, bass.ds(q * (TILES * TS) + t * TS, TS)].rearrange("p i s -> p s i"),
                             gx[:].rearrange("p (s i) -> p s i", i=F), gx_taken)
                    if s == H_OUT_SLOT:
                        uses += 1
                        act.wait_ge(gx_ready, gx_count(k, block_, uses))
                        copy(h1sum[:, bass.ds(k * SAMPLES, SAMPLES)], gx[:, 0:SAMPLES], gx_taken)
                    if layer0 and s == HIGH0_SLOT:
                        act.wait_ge(z_used, k * NT0 + 2 * NT0)
                        act.wait_ge(y_ready, k * SLOTS + 3 * QUADS)
                        high(k + 1, 0)

            def phase(block_):
                uses = GX_END if isinstance(block_, int) else gx_count(block_ * BLOCK + BLOCK, block_, 1)
                act.wait_ge(gx_ready, uses)
                copy(h2sum[:, bass.ds(block_ * P, P)], gx[:, 0:P], gx_taken)

            in_loops(act, group, phase)
            act.wait_ge(gx_ready, GX_END + 1)
            copy(gbuf[:, :, 0:TS].rearrange("p i s -> p s i"), gx[:].rearrange("p (s i) -> p s i", i=F), gx_taken)
            act.wait_ge(gx_ready, GX_END + 2)
            copy(h1sum[:, B:B + SAMPLES], gx[:, 0:SAMPLES], gx_taken)
            act.wait_ge(gx_ready, GX_END + 3)
            copy(h2sum[:, B:B + TS], gx[:, 0:TS], gx_taken)

        @block.vector
        def _(dve):
            def product(g, n):
                kb, a = TILES0[n]
                if a == 0:
                    dve.wait_ge(rotb_in[kb], g * 32 + 32)
                elif kb == 0:
                    dve.wait_ge(rota_in[a], g * 32 + 32)
                if not (isinstance(g, int) and g == 0 and n < ZBUFS):
                    dve.wait_ge(z_used, g * NT0 + max(0, n - ZBUFS + 1))
                nc.vector.tensor_tensor(z[:, n % ZBUFS, :], rotb[:, kb, :], rota[:, a, :], ALU.mult).then_inc(z_ready, 1)

            def low(g, part):
                cols = slice(0, 3 * P) if part == 0 else slice(3 * P, COLS)
                dve.wait_ge(h0_hi_ready, g * 2 + (part + 1 + LEAD))
                nc.vector.tensor_tensor(h0_lo[:, cols], l0acc[:, cols], h0_hi[:, cols].bitcast(F32),
                                        ALU.subtract).then_inc(h0_lo_ready, 1)

            def sum_depths(g):
                nc.vector.tensor_reduce(h0sum[:, bass.ds(g * SAMPLES, SAMPLES)], l0acc[:].rearrange("p (s d) -> p s d", d=D),
                                        AX.X, ALU.add).then_inc(h0_summed, 1)

            def scalars(t):
                nc.vector.tensor_copy(xs[:, t, :], xnext[:, t, :]).then_inc(xs_ready, 1)

            for s in (h0_lo_ready, h0_summed, xs_ready, fold, z_ready):
                nc.vector.sem_inc(s, LEAD)
            nc.vector.memset(h1[:], 0.0).then_inc(zeroed, 1)
            nc.vector.memset(acc_d[:], 0.0).then_inc(zeroed, 1)
            nc.vector.memset(acc_p[:], 0.0).then_inc(zeroed, 1)
            dve.wait_ge(zeroed, 3)
            nc.vector.sem_inc(dve_half, 2 * AHEAD_D)
            dve.wait_ge(w0_in, 32)
            nc.vector.tensor_tensor(w0[0:F, 0, :], w0[0:F, 0, :], w0b_sb[0:F, 0, :], ALU.add)
            nc.vector.tensor_tensor(w0[F:P, NT0 - 1, :], w0[F:P, NT0 - 1, :], w0b_sb[F:P, NT0 - 1, :], ALU.add)
            nc.vector.tensor_tensor(w0[:, 1:ROTA - 1, :], w0[:, 1:ROTA - 1, :], w0b_sb[:, 1:ROTA - 1, :], ALU.add)
            nc.vector.tensor_tensor(w0[:, ROTA:NT0 - 1, :], w0[:, ROTA:NT0 - 1, :], w0b_sb[:, ROTA:NT0 - 1, :],
                                    ALU.add).then_inc(w0_ready, 1)

            def w1_low(c):
                cols = slice(c * CH * N, (c + 1) * CH * N)
                dve.wait_ge(w1_hi_ready, c + 1)
                nc.vector.tensor_tensor(w1_lo[:, cols], stage[c % 2].rearrange("p i n -> p (i n)"), w1_hi[:, cols].bitcast(F32),
                                        ALU.subtract).then_inc(w1_lo_ready, 1)

            for c in range(F // CH):
                w1_low(c)
            for n in range(NT0):
                product(0, n)
            dve.wait_ge(first_x_out, 1)
            for t in range(TILES - 1):
                scalars(t)
            low(0, 0)

            def fold_step(k, t, step):
                par, acc, slot = (t + 1) % 2, acc_d[:, (t + 1) % 2, :], (t - 1) % TILES
                if step == 0:
                    dve.wait_ge(pool_add, adds_done(k, t * ADDS))
                    dve.wait_ge(dve_half, halves_done(k, t * ND))
                    nc.vector.tensor_tensor(acc, acc, acc_p[:, par, :], ALU.add).then_inc(fold, 1)
                elif step == 1:
                    dve.wait_ge(fold, folds_done(k, 3 * t + 1))
                    nc.vector.tensor_tensor(acc[:, 0:2 * N], acc[:, 0:2 * N], acc[:, 2 * N:4 * N], ALU.add).then_inc(fold, 1)
                else:
                    dve.wait_ge(fold, folds_done(k, 3 * t + 2))
                    nc.vector.tensor_tensor(h1[:, slot, :], acc[:, 0:N], acc[:, N:2 * N], ALU.add).then_inc(fold, 1)

            def group(k, q_, block_, layer0):
                for s in range(SLOTS):
                    t, q = s // QUADS, s % QUADS
                    if q in DVE_QUADS:
                        j = DVE_QUADS.index(q)
                        dve.wait_ge(y_ready, k * SLOTS + (s + 1))
                        if j == 0:
                            dve.wait_ge(xs_ready, k * TILES + (t + 1 + LEAD))
                            dve.wait_ge(fold, folds_done(k, 3 * t))
                        for m in range(QUAD):
                            i = q * QUAD + m
                            part, out = yq[:, s % YBANKS, m * N:(m + 1) * N], acc_d[:, t % 2, m * N:(m + 1) * N]
                            if j == 0:
                                ins = nc.vector.tensor_scalar(out, part, xs[:, t, i:i + 1], None, ALU.mult)
                            else:
                                if m % 2 == 0:
                                    dve.wait_ge(dve_half, halves_done(k, t * ND + j - 1) + (m // 2 + 1))
                                ins = nc.vector.scalar_tensor_tensor(out=out, in0=part, scalar=xs[:, t, i:i + 1], in1=out,
                                                                     op0=ALU.mult, op1=ALU.add)
                            if m % 2 == 1:
                                ins.then_inc(dve_half, 1)
                    if s == XS3_SLOT:
                        dve.wait_ge(act_quad, act_done(k, 0))
                        dve.wait_ge(dve_half, halves_done(k, 0))
                        dve.wait_ge(bd_ready, k * TILES + LEAD)
                        scalars(TILES - 1)
                    if s == LOW_SLOT:
                        low(k, 1)
                    if s == SUM_SLOT:
                        sum_depths(k)
                    if q in FOLD_AFTER:
                        if FOLD_AFTER[q] == 2:
                            dve.wait_ge(gx_ready, gx_count(k, block_, 0) if t == 0 else gx_count(k, block_, (3 if layer0 else 2) + t - 1))
                        fold_step(k, t, FOLD_AFTER[q])
                    if layer0:
                        for n in range(NT0):
                            if s == Z_SLOT[n]:
                                product(k + 1, n)
                        if t == TILES - 1 and q in COPY_SLOT:
                            c = COPY_SLOT[q]
                            dve.wait_ge(act_quad, act_done(k, (c + 1) * NA))
                            dve.wait_ge(dve_half, halves_done(k, (c + 1) * ND))
                            dve.wait_ge(bd_ready, k * TILES + (c + 1 + LEAD))
                            dve.wait_ge(gx_taken, gx_count(k, block_, 1))
                            scalars(c)
                        if s == LOW0_SLOT:
                            low(k + 1, 0)

            in_loops(dve, group, lambda block_: None)
            dve.wait_ge(gx_ready, GX_END)
            for step in range(3):
                fold_step(GROUPS, 0, step)

        @block.tensor
        def _(pe):
            def turn(g, taken):
                pe.wait_ge(xt_in, g * 32 + 32)
                if taken is not None:
                    pe.wait_ge(gx_taken, taken)
                for t in range(TILES):
                    ins = nc.tensor.transpose(gx[:, t * P:(t + 1) * P], rota[:, 0, t * P:(t + 1) * P], ident[:])
                ins.then_inc(gx_ready, 1)

            def contract0(g, n):
                pe.wait_ge(z_ready, g * NT0 + (n + 1 + LEAD))
                if n == 0 and not (isinstance(g, int) and g == 0):
                    pe.wait_ge(h0_lo_ready, g * 2 + LEAD)
                    pe.wait_ge(h0_summed, g + LEAD)
                nc.tensor.matmul(l0acc[:], w0[:, n, :], z[:, n % ZBUFS, :], start=(n == 0), stop=(n == NT0 - 1)).then_inc(z_used, 1)

            def g_product(t):
                nc.tensor.matmul(gx[:], h1[:, (t - 1) % TILES, :], bd[:, (t + 1) % 2, :, :].rearrange("p s i -> p (s i)"),
                                 start=True, stop=True).then_inc(gx_ready, 1)

            def sum_h1():
                for t in range(TILES):
                    ins = nc.tensor.matmul(gx[:, t * TS:(t + 1) * TS], h1[:, t, :], mask_sb[:], start=True, stop=True)
                ins.then_inc(gx_ready, 1)

            pe.wait_ge(consts_in, 32)
            turn(0, None)
            pe.wait_ge(w0_ready, 1)
            for n in range(NT0):
                contract0(0, n)
            pe.wait_ge(w1_lo_ready, F // CH)
            pe.wait_ge(zeroed, 3)
            pe.wait_ge(first_x_out, 1)
            pe.wait_ge(bd_zeroed, 1)

            def group(k, q_, block_, layer0):
                uses = 0
                for s in range(SLOTS):
                    t, q = s // QUADS, s % QUADS
                    if q == 0:
                        pe.wait_ge(h0_lo_ready, k * 2 + (LEAD + (1 if t < TILES - 1 else 2)))
                    before = s - YBANKS
                    if before % QUADS in DVE_QUADS:
                        pe.wait_ge(dve_half, halves_done(k, quads_before(DVE_QUADS, before + 1)))
                    else:
                        pe.wait_ge(act_quad, act_done(k, quads_before(ACT_QUADS, before + 1)))
                    lhs = slice(t * P, (t + 1) * P)
                    rhs = slice(q * QUAD * N, (q + 1) * QUAD * N)
                    bank = yq[:, s % YBANKS, :]
                    nc.tensor.matmul(bank, h0_hi[:, lhs], w1_hi[:, rhs], start=True, stop=False)
                    nc.tensor.matmul(bank, h0_hi[:, lhs], w1_lo[:, rhs], start=False, stop=False)
                    nc.tensor.matmul(bank, h0_lo[:, lhs], w1_hi[:, rhs], start=False, stop=True).then_inc(y_ready, 1)
                    if layer0:
                        if s == XT_SLOT:
                            turn(k + 1, gx_count(k, block_, uses))
                            uses += 1
                        for n in range(NT0):
                            if s == L0_SLOT[n]:
                                contract0(k + 1, n)
                    if q == G_SLOT:
                        pe.wait_ge(gx_taken, gx_count(k, block_, uses))
                        pe.wait_ge(fold, folds_done(k, 3 * t + 3))
                        pe.wait_ge(bd_ready, k * TILES + (t + LEAD))
                        g_product(t)
                        uses += 1
                    if s == H_SLOT:
                        pe.wait_ge(gx_taken, gx_count(k, block_, uses))
                        sum_h1()
                        uses += 1

            def phase(block_):
                taken = GX_END - 1 if isinstance(block_, int) else gx_count(block_ * BLOCK + BLOCK, block_, 0)
                pe.wait_ge(w2_in, 16)
                pe.wait_ge(gx_taken, taken)
                layer2(P)

            def layer2(samples):
                for i in range(F):
                    ins = nc.tensor.matmul(gx[:, 0:samples], w2_sb[:, i, :], gbuf[:, i, 0:samples], start=(i == 0), stop=(i == F - 1))
                ins.then_inc(gx_ready, 1)

            in_loops(pe, group, phase)
            pe.wait_ge(gx_taken, GX_END)
            pe.wait_ge(fold, folds_done(GROUPS, 3))
            pe.wait_ge(bd_ready, GROUPS * TILES + LEAD)
            g_product(0)
            pe.wait_ge(gx_taken, GX_END + 1)
            sum_h1()
            pe.wait_ge(gx_taken, GX_END + 2)
            layer2(TS)


def mlp(nc, keep, dense, wt1, bt1, wt2, bt2, wt3, y):
    with ExitStack() as ctx:
        def sb(name, shape, dt=F32):
            return ctx.enter_context(nc.sbuf_tensor(name, shape, dt))

        def sem(name):
            return ctx.enter_context(nc.semaphore(name))

        H1, H2, Q = 512, 256, B // P
        dense_sb = sb("dense_sb", [P, Q, D])
        wt1_sb = sb("wt1_sb", [P, 3, H1])
        wt1d_sb = sb("wt1d_sb", [D, H1])
        wt2_sb = sb("wt2_sb", [P, H1 // P, H2])
        wt3_sb = sb("wt3_sb", [P, H2 // P])
        bt1_sb = sb("bt1_sb", [P, H1 // P])
        bt2_sb = sb("bt2_sb", [P, H2 // P])
        dense_t = sb("dense_t", [D, B])
        hid1 = sb("hid1", [P, H1 // P, B])
        hid2 = sb("hid2", [P, H2 // P, B])
        y_sb = sb("y_sb", [1, B])
        ps = ctx.enter_context(nc.psum_tensor("ps", [P, 8, B], F32))
        wt1_in = sem("wt1_in")
        rest_in = sem("rest_in")
        small_in = sem("small_in")
        dense_turned = sem("dense_turned")
        dense_ready = sem("dense_ready")
        lin1 = sem("lin1")
        hid1_ready = sem("hid1_ready")
        lin2 = sem("lin2")
        hid2_ready = sem("hid2_ready")
        lin3 = sem("lin3")
        y_in_sbuf = sem("y_in_sbuf")
        y_out = sem("y_out")
        block = ctx.enter_context(nc.Block())

        @block.sync
        def _(sp):
            sp.dma_start(wt1_sb[:], wt1[0:3 * P, :].rearrange("(k p) f -> p k f", p=P)).then_inc(wt1_in, 16)
            sp.dma_start(wt1d_sb[:], wt1[3 * P:3 * P + D, :]).then_inc(wt1_in, 16)
            sp.dma_start(wt2_sb[:], wt2.rearrange("(k p) f -> p k f", p=P)).then_inc(rest_in, 16)
            sp.wait_ge(y_in_sbuf, 1)
            sp.dma_start(y.rearrange("b o -> o b"), y_sb[:]).then_inc(y_out, 16)
            sp.wait_ge(y_out, 16)

        @block.scalar
        def _(act):
            act.dma_start(dense_sb[:], dense.rearrange("(b p) d -> p b d", p=P)).then_inc(small_in, 16)
            with nc.allow_non_contiguous_dma(reason="a few hundred words"):
                act.dma_start(bt1_sb[:], bt1.rearrange("(k p) -> p k", p=P)).then_inc(small_in, 16)
                act.dma_start(bt2_sb[:], bt2.rearrange("(k p) -> p k", p=P)).then_inc(small_in, 16)
                act.dma_start(wt3_sb[:], wt3.rearrange("(k p) o -> p (k o)", p=P)).then_inc(small_in, 16)
            act.wait_ge(dense_turned, 1)
            nc.scalar.activation(dense_t[:], ps[0:D, 7, :], ACT.Copy).then_inc(dense_ready, 1)
            for m in range(H1 // P):
                act.wait_ge(lin1, m + 1)
                nc.scalar.activation(hid1[:, m, :], ps[:, m, :], ACT.Relu, bias=bt1_sb[:, m:m + 1]).then_inc(hid1_ready, 1)
            for m in range(H2 // P):
                act.wait_ge(lin2, m + 1)
                nc.scalar.activation(hid2[:, m, :], ps[:, 4 + m, :], ACT.Relu, bias=bt2_sb[:, m:m + 1]).then_inc(hid2_ready, 1)

        @block.vector
        def _(dve):
            dve.wait_ge(lin3, 1)
            nc.vector.tensor_copy(y_sb[:], ps[0:1, 6, :]).then_inc(y_in_sbuf, 1)

        @block.tensor
        def _(pe):
            pe.wait_ge(small_in, 64)
            for c in range(Q):
                ins = nc.tensor.transpose(ps[0:D, 7, c * P:(c + 1) * P], dense_sb[:, c, :], keep["ident"][:])
            ins.then_inc(dense_turned, 1)
            pe.wait_ge(wt1_in, 32)
            for m in range(H1 // P):
                cols = slice(m * P, (m + 1) * P)
                terms = [(wt1_sb[:, 0, cols], keep["h0sum"][:]), (wt1_sb[:, 1, cols], keep["h1sum"][:, SAMPLES:]),
                         (wt1_sb[:, 2, cols], keep["h2sum"][:, TS:]), (wt1d_sb[:, cols], dense_t[:])]
                for n, (w, x) in enumerate(terms):
                    if m == 0 and n == 3:
                        pe.wait_ge(dense_ready, 1)
                    ins = nc.tensor.matmul(ps[:, m, :], w, x, start=(n == 0), stop=(n == 3))
                ins.then_inc(lin1, 1)
            pe.wait_ge(rest_in, 16)
            for m in range(H2 // P):
                for n in range(H1 // P):
                    pe.wait_ge(hid1_ready, n + 1)
                    ins = nc.tensor.matmul(ps[:, 4 + m, :], wt2_sb[:, n, m * P:(m + 1) * P], hid1[:, n, :],
                                           start=(n == 0), stop=(n == H1 // P - 1))
                ins.then_inc(lin2, 1)
            for m in range(H2 // P):
                pe.wait_ge(hid2_ready, m + 1)
                ins = nc.tensor.matmul(ps[0:1, 6, :], wt3_sb[:, m:m + 1], hid2[:, m, :], start=(m == 0), stop=(m == H2 // P - 1))
            ins.then_inc(lin3, 1)


def kernel(**inputs):
    import concourse.bacc as _bacc
    from concourse.bass_utils import run_bass_kernel_spmd as _run

    a = {name: np.ascontiguousarray(x) for name, x in inputs.items()}
    tables = np.concatenate([a[f"tbl_{f}"] for f in range(F)], axis=0)
    starts = np.cumsum([0] + [a[f"tbl_{f}"].shape[0] for f in range(F - 1)]).astype(np.int32)
    id_base = np.repeat(starts.reshape(TILES, D), SAMPLES, axis=0)
    part = np.arange(P)
    shift = np.stack([2 * kb + (part < F) for kb in range(ROTB)], 1)
    first = np.stack([(part + 8 * r) % F for _, r in TILES0], 1)
    second = np.stack([(part - shift[:, kb]) % F for kb, _ in TILES0], 1)
    w0 = a["L0_rec_W0"]
    mask = (part[:, None] // D == np.arange(TS)).astype(np.float32)
    arrays = {
        "tables": tables, "ids": a["ids"], "id_base": id_base, "mask": mask, "eye": np.eye(P, dtype=np.float32),
        "w0a": w0[first * F + second], "w0b": w0[second * F + first], "w1": a["L0_rec_W1"], "w2": a["L0_rec_W2"],
        "dense": a["dense_ctx"], "wt1": a["W_top1"], "bt1": a["b_top1"], "wt2": a["W_top2"], "bt2": a["b_top2"], "wt3": a["W_top3"],
    }
    nc = _bacc.Bacc("TRN2", target_bir_lowering=False, num_devices=1)
    args = [nc.dram_tensor(f"{n}_dram", x.shape, mybir.dt.from_np(x.dtype), kind="ExternalInput").ap() for n, x in arrays.items()]
    args.append(nc.dram_tensor("y_dram", (B, 1), F32, kind="ExternalOutput").ap())
    dlrm(nc, *args)
    r = _run(nc, [{f"{n}_dram": x for n, x in arrays.items()}], core_ids=[0])
    return r.results[0]["y_dram"]
```

```python
from contextlib import ExitStack

import numpy as np

import concourse.bass as bass
from concourse import mybir

ALU = mybir.AluOpType
ACT = mybir.ActivationFunctionType
AX = mybir.AxisListType
F32 = mybir.dt.float32
F32R = mybir.dt.float32r
I32 = mybir.dt.int32

P = 128
B = 512
F = 64
D = 16
N = 128
COLS = 512
SAMPLES = COLS // D
GROUPS = B // SAMPLES
TILES = COLS // P
TS = P // D
BLOCK = 4
BLOCKS = GROUPS // BLOCK
H1, H2 = 512, 256

QUAD = 4
QUADS = F // QUAD
SLOTS = TILES * QUADS
YBANKS = 4

ROTA = 5
ROTB = 4
TILES0 = [(kb, a) for kb in range(ROTB) for a in range(ROTA if kb == 0 else ROTA - 1)]
NT0 = len(TILES0)
ZBUFS = 3
ZHBUFS = 2
UNSPLIT = range(0, NT0, 4)
SPLIT = [n for n in range(NT0) if n not in UNSPLIT]
NSPLIT = len(SPLIT)

MIXED = [6, 12]
DVE_QUADS = [q for q in range(QUADS) if q % 2 == 0]
ACT_QUADS = [q for q in range(QUADS) if q % 2 == 1 or q in MIXED]
POOL_QUADS = [q for q in range(QUADS) if q % 2 == 1][1:]
ND, NA, ADDS = len(DVE_QUADS), len(ACT_QUADS), len(POOL_QUADS)
TMPS = 3
FOLD_AFTER = {DVE_QUADS[1]: 0, DVE_QUADS[3]: 1, DVE_QUADS[4]: 2}

HIGH_SLOT = 5
LOW_SLOT = 7
XS3_SLOT = 4
XT_SLOT = 8
X_OUT_SLOT = 9
L0_SLOT = [16 + (n * 43) // (NT0 - 1) for n in range(NT0)]
Z_SLOT = [s - 8 for s in L0_SLOT]
ZHI_SLOT = [s - 6 for s in L0_SLOT]
ZLO_SLOT = [s - 4 for s in L0_SLOT]
COPY_SLOT = {2: 0, 3: 1, 4: 2}
HIGH0_SLOT = 60
LOW0_SLOT = 61
SUM_SLOT = 9
H0SUM_OUT_SLOT = 21
G_SLOT = 13
G_OUT_SLOT = 14
H_SLOT = 18
H_OUT_SLOT = 19
GX_USES = 2 + TILES
LEAD = 1
GX_END = GROUPS * GX_USES + BLOCKS - 2 + LEAD


def quads_before(quads, slot):
    return slot // QUADS * len(quads) + sum(q < slot % QUADS for q in quads)


AHEAD_D = LEAD - quads_before(DVE_QUADS, 1 - YBANKS)
AHEAD_A = LEAD - quads_before(ACT_QUADS, 1 - YBANKS)


def halves_done(k, quads):
    return k * (2 * TILES * ND) + 2 * (quads + AHEAD_D)


def act_done(k, quads):
    return k * (TILES * NA) + (quads + AHEAD_A)


def adds_done(k, adds):
    return k * (TILES * ADDS) + (adds + LEAD)


def folds_done(k, folds):
    return k * (3 * TILES) + (folds + LEAD)


def gx_count(k, block, uses):
    return k * GX_USES + block + (uses + LEAD)


def tmp_slot(t, a):
    return (t * (NA - 1) + a - 1) % TMPS


def in_loops(eng, group, phase):
    with eng.Fori(0, BLOCKS - 1, 1) as block:
        with eng.Fori(0, BLOCK, 1) as q:
            group(eng.snap(block * BLOCK + q), q, block, True)
        phase(block)
    last = BLOCKS - 1
    with eng.Fori(0, BLOCK - 1, 1) as q:
        group(eng.snap(q + last * BLOCK), q, last, True)
    group(GROUPS - 1, BLOCK - 1, last, False)


def dlrm(nc, tables, ids, id_base, mask, eye, w0a, w0b, w1, w2, dense, wt1, bt1, wt2, bt2, wt3, y):
    h0sum_dram = nc.dram_tensor("h0sum_scratch", (P, B), F32, kind="Internal").ap()
    x_dram = nc.dram_tensor("x_scratch", (GROUPS, F, COLS), F32, kind="Internal").ap()
    with ExitStack() as ctx:
        def sb(name, shape, dt=F32):
            return ctx.enter_context(nc.sbuf_tensor(name, shape, dt))

        def psum(name, shape):
            return ctx.enter_context(nc.psum_tensor(name, shape, F32))

        def sem(name):
            return ctx.enter_context(nc.semaphore(name))

        h0sum = sb("h0sum", [P, SAMPLES])
        h1sum = sb("h1sum", [P, SAMPLES + B])
        h2sum = sb("h2sum", [P, TS + B])
        ident = sb("ident", [P, P])
        rota = sb("rota", [P, ROTA, COLS])
        rotb = sb("rotb", [P, ROTB, COLS])
        w1_hi = sb("w1_hi", [P, F * N], F32R)
        w1_lo = sb("w1_lo", [P, F * N], F32R)
        w2_sb = sb("w2_sb", [P, F, N])
        w0 = sb("w0", [P, NT0 - NSPLIT, N])
        w0_hi = sb("w0_hi", [P, NSPLIT, N], F32R)
        w0_lo = sb("w0_lo", [P, NSPLIT, N], F32R)
        gbuf = sb("gbuf", [P, F, P + TS])
        base_sb = sb("base_sb", [P, D], I32)
        idx = sb("idx", [P, (GROUPS + 1) * D], I32)
        idx_now = sb("idx_now", [P, D], I32)
        raw = sb("raw", [P, D * D])
        xnext = sb("xnext", [P, TILES, F])
        xs = sb("xs", [P, TILES, F])
        mask_sb = sb("mask_sb", [P, TS])
        bd = sb("bd", [P, TS, F])
        z = sb("z", [P, ZBUFS, COLS])
        z_hi = sb("z_hi", [P, ZHBUFS, COLS], F32R)
        z_lo = sb("z_lo", [P, ZHBUFS, COLS], F32R)
        h0_hi = sb("h0_hi", [P, COLS], F32R)
        h0_lo = sb("h0_lo", [P, COLS], F32R)
        tmp = sb("tmp", [P, TMPS, QUAD * N])
        acc_d = sb("acc_d", [P, 2, QUAD * N])
        acc_p = sb("acc_p", [P, 2, QUAD * N])
        h1 = sb("h1", [P, TILES, N])

        yq = psum("yq", [P, YBANKS, QUAD * N])
        l0acc = psum("l0acc", [P, COLS])
        gx = psum("gx", [P, COLS])

        ids_in = sem("ids_in")
        idx_ready = sem("idx_ready")
        consts_in = sem("consts_in")
        w0_in = sem("w0_in")
        w0_summed = sem("w0_summed")
        w0_hi_ready = sem("w0_hi_ready")
        w0_ready = sem("w0_ready")
        w1_in = [sem("w1_in0"), sem("w1_in1")]
        w1_hi_ready = sem("w1_hi_ready")
        w1_lo_ready = sem("w1_lo_ready")
        w2_in = sem("w2_in")
        looked_up = sem("looked_up")
        idx_staged = sem("idx_staged")
        x_written = sem("x_written")
        xt_in = sem("xt_in")
        rotb_in = [sem(f"rotb_in{kb}") for kb in range(ROTB)]
        rota_in = [None] + [sem(f"rota_in{a}") for a in range(1, ROTA)]
        z_ready = sem("z_ready")
        z_used = sem("z_used")
        z_hi_ready = sem("z_hi_ready")
        z_lo_ready = sem("z_lo_ready")
        h0_hi_ready = sem("h0_hi_ready")
        h0_lo_ready = sem("h0_lo_ready")
        h0_summed = sem("h0_summed")
        h0sum_out = sem("h0sum_out")
        xs_ready = sem("xs_ready")
        bd_ready = sem("bd_ready")
        y_ready = sem("y_ready")
        dve_half = sem("dve_half")
        act_quad = sem("act_quad")
        pool_add = sem("pool_add")
        fold = sem("fold")
        gx_ready = sem("gx_ready")
        gx_taken = sem("gx_taken")
        zeroed = sem("zeroed")
        first_x_out = sem("first_x_out")
        bd_zeroed = sem("bd_zeroed")
        weights_in = sem("weights_in")
        dense_turned = sem("dense_turned")
        dense_ready = sem("dense_ready")
        lin1 = sem("lin1")
        hid1_ready = sem("hid1_ready")
        lin2 = sem("lin2")
        hid2_ready = sem("hid2_ready")
        lin3 = sem("lin3")
        y_in_sbuf = sem("y_in_sbuf")
        y_out = sem("y_out")

        a_flat, b_flat = rota[:].rearrange("p a c -> p (a c)"), rotb[:].rearrange("p a c -> p (a c)")
        small = H1 + B + B // P * D
        wt1_sb = a_flat[:, 0:3 * H1].rearrange("p (k f) -> p k f", f=H1)
        wt2_sb = a_flat[:, 3 * H1:3 * H1 + H1 // P * H2].rearrange("p (k f) -> p k f", f=H2)
        wt1d_sb = b_flat[0:D, 0:H1]
        dense_t = b_flat[0:D, H1:H1 + B]
        dense_sb = b_flat[:, H1 + B:small].rearrange("p (b d) -> p b d", d=D)
        bt1_sb = b_flat[:, small:small + H1 // P]
        bt2_sb = b_flat[:, small + H1 // P:small + (H1 + H2) // P]
        wt3_sb = b_flat[:, small + (H1 + H2) // P:small + (H1 + 2 * H2) // P]
        h0_all = b_flat[:, small + (H1 + 2 * H2) // P:small + (H1 + 2 * H2) // P + B]
        hid1 = [acc_d[:, 0, :], acc_d[:, 1, :], acc_p[:, 0, :], acc_p[:, 1, :]]
        hid2 = [z[:, 0, :], z[:, 1, :]]
        y_sb = z[0:1, 2, :]
        lin2_bank = [gx, l0acc]

        w1_view = w1.rearrange("(i j) n -> j i n", j=P)
        w2_view = w2.rearrange("(i j) n -> j i n", j=P)
        start = gbuf[:].rearrange("p i b -> p (i b)")
        w0a_sb = start[:, 0:NT0 * N].rearrange("p (t n) -> p t n", n=N)
        w0_to_split = w0a_sb[:, 1:NT0, :].rearrange("p (g r) n -> p g r n", r=4)[:, :, 0:3, :]
        w0b_sb = start[:, NT0 * N:2 * NT0 * N].rearrange("p (t n) -> p t n", n=N)
        ids_sb = start[:, 2 * NT0 * N:2 * NT0 * N + GROUPS * D].bitcast(I32)
        CH = F // 4
        stage = [w2_sb[:, 0:CH, :], w2_sb[:, CH:2 * CH, :]]
        block = ctx.enter_context(nc.Block())

        def by_three(w):
            return w.rearrange("p (g r) n -> p g r n", r=3)

        @block.sync
        def _(sp):
            for r in range(TILES):
                rows = slice(r * SAMPLES, (r + 1) * SAMPLES)
                sp.dma_start(ids_sb[rows, :].rearrange("s (g f) -> s g f", f=D),
                             ids[:, r * D:(r + 1) * D].rearrange("(g s) f -> s g f", s=SAMPLES)).then_inc(ids_in, 16)
            sp.dma_start(base_sb[:], id_base).then_inc(ids_in, 16)
            sp.dma_start(ident[:], eye).then_inc(consts_in, 16)
            sp.dma_start(mask_sb[:], mask).then_inc(consts_in, 16)
            sp.dma_start(w0a_sb, w0a).then_inc(w0_in, 16)
            sp.dma_start(w0b_sb, w0b).then_inc(w0_in, 16)
            for c in range(2):
                sp.dma_start(stage[c], w1_view[:, c * CH:(c + 1) * CH, :]).then_inc(w1_in[c], 16)

            def bring(g, z_done):
                sp.wait_ge(looked_up, g * (16 * D) + 16 * D)
                dst = x_dram[bass.ds(g, 1), :, :].rearrange("o (r f) (s d) -> (o r) s f d", f=D, d=D)
                for r in range(TILES):
                    sp.dma_start(dst[r], raw[r * SAMPLES:(r + 1) * SAMPLES, :].rearrange("s (f d) -> s f d", d=D)).then_inc(x_written, 16)
                sp.wait_ge(x_written, g * (16 * TILES) + 16 * TILES)
                if z_done is not None:
                    sp.wait_ge(z_ready, z_done)
                for h in range(2):
                    sp.dma_start(rota[h * F:(h + 1) * F, 0, :], x_dram[bass.ds(g, 1), :, :].rearrange("o f c -> (o f) c")).then_inc(xt_in, 16)
                sp.wait_ge(xt_in, g * 32 + 32)
                for kb in range(ROTB):
                    for h in range(2):
                        first = F - 2 * kb - (1 - h)
                        sp.dma_start(rotb[h * F:(h + 1) * F, kb, :], rota[first:first + F, 0, :]).then_inc(rotb_in[kb], 16)
                    for a in range(1, ROTA) if kb == 0 else ():
                        for h in range(2):
                            sp.dma_start(rota[h * F:(h + 1) * F, a, :], rota[8 * a:8 * a + F, 0, :]).then_inc(rota_in[a], 16)

            bring(0, None)
            bring(1, NT0 + LEAD)
            sp.wait_ge(w1_lo_ready, F // CH)
            sp.dma_start(w2_sb[:], w2_view).then_inc(w2_in, 16)
            with sp.Fori(1, GROUPS - 1, 1) as k:
                bring(k + 1, k * NT0 + (NT0 + LEAD))
            sp.wait_ge(z_ready, GROUPS * NT0 + LEAD)
            sp.dma_start(dense_sb, dense.rearrange("(b p) d -> p b d", p=P)).then_inc(weights_in, 16)
            sp.dma_start(wt1_sb, wt1[0:3 * P, :].rearrange("(k p) f -> p k f", p=P)).then_inc(weights_in, 16)
            sp.dma_start(wt1d_sb, wt1[3 * P:3 * P + D, :]).then_inc(weights_in, 16)
            sp.dma_start(wt2_sb, wt2.rearrange("(k p) f -> p k f", p=P)).then_inc(weights_in, 16)
            with nc.allow_non_contiguous_dma(reason="a few hundred words"):
                sp.dma_start(bt1_sb, bt1.rearrange("(k p) -> p k", p=P)).then_inc(weights_in, 16)
                sp.dma_start(bt2_sb, bt2.rearrange("(k p) -> p k", p=P)).then_inc(weights_in, 16)
                sp.dma_start(wt3_sb, wt3.rearrange("(k p) o -> p (k o)", p=P)).then_inc(weights_in, 16)
            sp.wait_ge(h0sum_out, GROUPS * 16 + LEAD)
            sp.dma_start(h0_all, h0sum_dram).then_inc(weights_in, 16)
            sp.wait_ge(y_in_sbuf, 1)
            sp.dma_start(y.rearrange("b o -> o b"), y_sb).then_inc(y_out, 16)
            sp.wait_ge(y_out, 16)

        def lookups(first, last):
            for f in range(first, last):
                nc.gpsimd.indirect_dma_start(out=raw[:, f * D:(f + 1) * D], out_offset=None, in_=tables,
                                             in_offset=bass.IndirectOffsetOnAxis(ap=idx_now[:, f:f + 1], axis=0)).then_inc(looked_up, 16)

        @block.gpsimd
        def _(pool):
            def stage_idx(g):
                nc.gpsimd.tensor_copy(idx_now[:], idx[:, bass.ds(g * D, D)]).then_inc(idx_staged, 1)
                pool.wait_ge(idx_staged, g + 1)

            for s in (pool_add, bd_ready):
                nc.gpsimd.sem_inc(s, LEAD)
            nc.gpsimd.memset(idx[:, GROUPS * D:], 0)
            pool.wait_ge(ids_in, 16 * (TILES + 1))
            nc.gpsimd.tensor_tensor(idx[:, 0:GROUPS * D].rearrange("p (g f) -> p g f", f=D), ids_sb.rearrange("p (g f) -> p g f", f=D),
                                    base_sb[:].unsqueeze(1).to_broadcast([P, GROUPS, D]), ALU.add).then_inc(idx_ready, 1)
            pool.wait_ge(idx_ready, 1)
            stage_idx(0)
            lookups(0, D)
            nc.gpsimd.memset(bd[:], 0.0).then_inc(bd_zeroed, 1)
            pool.wait_ge(x_written, 16 * TILES)
            stage_idx(1)
            lookups(0, D)
            pool.wait_ge(bd_zeroed, 1)
            pool.wait_ge(zeroed, 3)
            pool.wait_ge(consts_in, 32)

            def group(k, q, block_, layer0):
                given = 0
                for t in range(TILES):
                    if layer0 and t == 0:
                        pool.wait_ge(x_written, k * (16 * TILES) + 2 * 16 * TILES)
                        stage_idx(k + 2)
                    for a, quad in enumerate(POOL_QUADS, 1):
                        scaled = ACT_QUADS.index(quad)
                        pool.wait_ge(act_quad, act_done(k, t * NA + scaled + 1))
                        if a > 1:
                            pool.wait_ge(pool_add, adds_done(k, t * ADDS + a - 1))
                        acc = acc_p[:, t % 2, :]
                        nc.gpsimd.tensor_tensor(acc, acc, tmp[:, tmp_slot(t, scaled), :], ALU.add).then_inc(pool_add, 1)
                        if a == ADDS:
                            pool.wait_ge(xs_ready, k * TILES + (t + 1 + LEAD))
                            pool.wait_ge(gx_ready, gx_count(k, block_, ([2, 4, 5, 6] if layer0 else [1, 3, 4, 5])[t]))
                            nc.gpsimd.tensor_tensor(bd[:], xs[:, t:t + 1, :].to_broadcast([P, TS, F]),
                                                    mask_sb[:].unsqueeze(2).to_broadcast([P, TS, F]), ALU.mult).then_inc(bd_ready, 1)
                        upto = min(D, -(-(t * ADDS + a) * D // ((TILES - 1) * ADDS)))
                        if layer0 and upto > given:
                            lookups(given, upto)
                            given = upto

            in_loops(pool, group, lambda block_: None)
            pool.wait_ge(looked_up, (GROUPS + 1) * 16 * D)

        @block.scalar
        def _(act):
            def copy(out, in_, done):
                nc.scalar.activation(out, in_, ACT.Copy).then_inc(done, 1)

            def high(g, part):
                cols = slice(0, 3 * P) if part == 0 else slice(3 * P, COLS)
                copy(h0_hi[:, cols], l0acc[:, cols], h0_hi_ready)

            def z_high(g, n):
                act.wait_ge(z_ready, g * NT0 + (n + 1 + LEAD))
                i = SPLIT.index(n)
                act.wait_ge(z_used, g * NT0 + (SPLIT[i - ZHBUFS] + 1 if i >= ZHBUFS else 0))
                copy(z_hi[:, i % ZHBUFS, :], z[:, n % ZBUFS, :], z_hi_ready)

            def x_out(g, uses):
                act.wait_ge(gx_ready, uses)
                act.wait_ge(xs_ready, g * TILES + LEAD)
                copy(xnext[:], gx[:].rearrange("p (t h i) -> p t h i", h=2, i=F)[:, :, 0, :], gx_taken)

            for s in (gx_taken, h0_hi_ready, z_hi_ready, h0sum_out):
                nc.scalar.sem_inc(s, LEAD)
            nc.scalar.sem_inc(act_quad, AHEAD_A)
            act.wait_ge(w0_summed, 4)
            copy(by_three(w0_hi[:]), w0_to_split, w0_hi_ready)
            for c in range(2):
                act.wait_ge(w1_in[c], 16)
                copy(w1_hi[:, c * CH * N:(c + 1) * CH * N], stage[c].rearrange("p i n -> p (i n)"), w1_hi_ready)
            for c in range(2, F // CH):
                act.wait_ge(w1_lo_ready, c - 1)
                act.dma_start(stage[c % 2], w1_view[:, c * CH:(c + 1) * CH, :]).then_inc(w1_in[c % 2], 16)
            for c in range(2, F // CH):
                act.wait_ge(w1_in[c % 2], 32)
                copy(w1_hi[:, c * CH * N:(c + 1) * CH * N], stage[c % 2].rearrange("p i n -> p (i n)"), w1_hi_ready)
            act.wait_ge(gx_ready, 1)
            copy(xnext[:], gx[:].rearrange("p (t h i) -> p t h i", h=2, i=F)[:, :, 0, :], first_x_out)
            act.wait_ge(z_used, NT0)
            high(0, 0)

            def group(k, q, block_, layer0):
                uses = 0
                for s in range(SLOTS):
                    t, qd = s // QUADS, s % QUADS
                    if qd in ACT_QUADS:
                        a = ACT_QUADS.index(qd)
                        if a == 0:
                            act.wait_ge(xs_ready, k * TILES + (t + 1 + LEAD))
                            act.wait_ge(fold, folds_done(k, max(0, 3 * (t - 1) + 1)))
                            out = acc_p[:, t % 2, :]
                        else:
                            before = t * (NA - 1) + a - 1 - TMPS
                            if before < 0:
                                act.wait_ge(pool_add, adds_done(k, 0))
                                act.wait_ge(dve_half, halves_done(k, LEAD - AHEAD_D))
                            else:
                                tile, quad = before // (NA - 1), ACT_QUADS[before % (NA - 1) + 1]
                                if quad in MIXED:
                                    act.wait_ge(dve_half, halves_done(k, tile * ND + DVE_QUADS.index(quad) + 1))
                                else:
                                    act.wait_ge(pool_add, adds_done(k, tile * ADDS + POOL_QUADS.index(quad) + 1))
                            out = tmp[:, tmp_slot(t, a), :]
                        act.wait_ge(y_ready, k * SLOTS + (s + 1))
                        for m in range(QUAD):
                            i = qd * QUAD + m
                            ins = nc.scalar.activation(out[:, m * N:(m + 1) * N], yq[:, s % YBANKS, m * N:(m + 1) * N],
                                                       ACT.Copy, scale=xs[:, t, i:i + 1])
                        ins.then_inc(act_quad, 1)
                    if s == HIGH_SLOT:
                        act.wait_ge(h0_lo_ready, k * 2 + (1 + LEAD))
                        high(k, 1)
                    if layer0 and s == X_OUT_SLOT:
                        x_out(k + 1, gx_count(k, block_, 1))
                        uses += 1
                    if qd == G_OUT_SLOT:
                        uses += 1
                        act.wait_ge(gx_ready, gx_count(k, block_, uses))
                        copy(gbuf[:, :, bass.ds(q * (TILES * TS) + t * TS, TS)].rearrange("p i s -> p s i"),
                             gx[:].rearrange("p (s i) -> p s i", i=F), gx_taken)
                    if s == H_OUT_SLOT:
                        uses += 1
                        act.wait_ge(gx_ready, gx_count(k, block_, uses))
                        copy(h1sum[:, bass.ds(k * SAMPLES, SAMPLES)], gx[:, 0:SAMPLES], gx_taken)
                    for n in SPLIT if layer0 else ():
                        if s == ZHI_SLOT[n]:
                            z_high(k + 1, n)
                    if s == H0SUM_OUT_SLOT:
                        act.wait_ge(h0_summed, k + (1 + LEAD))
                        act.dma_start(h0sum_dram[:, bass.ds(k * SAMPLES, SAMPLES)], h0sum[:]).then_inc(h0sum_out, 16)
                    if layer0 and s == HIGH0_SLOT:
                        act.wait_ge(z_used, k * NT0 + 2 * NT0)
                        act.wait_ge(y_ready, k * SLOTS + 3 * QUADS)
                        high(k + 1, 0)

            def phase(block_):
                act.wait_ge(gx_ready, gx_count(block_ * BLOCK + BLOCK, block_, 1))
                copy(h2sum[:, bass.ds(block_ * P, P)], gx[:, 0:P], gx_taken)

            in_loops(act, group, phase)
            act.wait_ge(dense_turned, 1)
            copy(dense_t, l0acc[0:D, :], dense_ready)
            act.wait_ge(gx_ready, GX_END + 1)
            copy(gbuf[:, :, P:].rearrange("p i s -> p s i"), gx[:].rearrange("p (s i) -> p s i", i=F), gx_taken)
            act.wait_ge(gx_ready, GX_END + 2)
            copy(h1sum[:, B:B + SAMPLES], gx[:, 0:SAMPLES], gx_taken)
            act.wait_ge(gx_ready, GX_END + 3)
            copy(h2sum[:, B - P:], gx[:, 0:P + TS], gx_taken)
            act.wait_ge(weights_in, 16 * 8)
            for m in range(H1 // P):
                act.wait_ge(lin1, m + 1)
                nc.scalar.activation(hid1[m], yq[:, m, :], ACT.Relu, bias=bt1_sb[:, m:m + 1]).then_inc(hid1_ready, 1)
            for m in range(H2 // P):
                act.wait_ge(lin2, m + 1)
                nc.scalar.activation(hid2[m], lin2_bank[m][:], ACT.Relu, bias=bt2_sb[:, m:m + 1]).then_inc(hid2_ready, 1)

        @block.vector
        def _(dve):
            def product(g, n):
                kb, a = TILES0[n]
                if a == 0:
                    dve.wait_ge(rotb_in[kb], g * 32 + 32)
                elif kb == 0:
                    dve.wait_ge(rota_in[a], g * 32 + 32)
                if not (isinstance(g, int) and g == 0 and n < ZBUFS):
                    dve.wait_ge(z_used, g * NT0 + max(0, n - ZBUFS + 1))
                nc.vector.tensor_tensor(z[:, n % ZBUFS, :], rotb[:, kb, :], rota[:, a, :], ALU.mult).then_inc(z_ready, 1)

            def z_low(g, n):
                dve.wait_ge(z_hi_ready, (g - 1) * NSPLIT + (SPLIT.index(n) + 1 + LEAD))
                half = SPLIT.index(n) % ZHBUFS
                nc.vector.tensor_tensor(z_lo[:, half, :], z[:, n % ZBUFS, :], z_hi[:, half, :].bitcast(F32), ALU.subtract).then_inc(z_lo_ready, 1)

            def low(g, part):
                cols = slice(0, 3 * P) if part == 0 else slice(3 * P, COLS)
                dve.wait_ge(h0_hi_ready, g * 2 + (part + 1 + LEAD))
                nc.vector.tensor_tensor(h0_lo[:, cols], l0acc[:, cols], h0_hi[:, cols].bitcast(F32),
                                        ALU.subtract).then_inc(h0_lo_ready, 1)

            def sum_depths(g):
                dve.wait_ge(h0sum_out, g * 16 + LEAD)
                nc.vector.tensor_reduce(h0sum[:], l0acc[:].rearrange("p (s d) -> p s d", d=D),
                                        AX.X, ALU.add).then_inc(h0_summed, 1)

            def scalars(t):
                nc.vector.tensor_copy(xs[:, t, :], xnext[:, t, :]).then_inc(xs_ready, 1)

            for s in (h0_lo_ready, h0_summed, xs_ready, fold, z_ready, z_lo_ready):
                nc.vector.sem_inc(s, LEAD)
            nc.vector.memset(h1[:], 0.0).then_inc(zeroed, 1)
            nc.vector.memset(acc_d[:], 0.0).then_inc(zeroed, 1)
            nc.vector.memset(acc_p[:], 0.0).then_inc(zeroed, 1)
            dve.wait_ge(zeroed, 3)
            nc.vector.sem_inc(dve_half, 2 * AHEAD_D)
            dve.wait_ge(w0_in, 32)
            nc.vector.tensor_tensor(w0a_sb[0:F, 0, :], w0a_sb[0:F, 0, :], w0b_sb[0:F, 0, :], ALU.add).then_inc(w0_summed, 1)
            nc.vector.tensor_tensor(w0a_sb[F:P, NT0 - 1, :], w0a_sb[F:P, NT0 - 1, :], w0b_sb[F:P, NT0 - 1, :], ALU.add).then_inc(w0_summed, 1)
            nc.vector.tensor_tensor(w0a_sb[:, 1:ROTA - 1, :], w0a_sb[:, 1:ROTA - 1, :], w0b_sb[:, 1:ROTA - 1, :], ALU.add).then_inc(w0_summed, 1)
            nc.vector.tensor_tensor(w0a_sb[:, ROTA:NT0 - 1, :], w0a_sb[:, ROTA:NT0 - 1, :], w0b_sb[:, ROTA:NT0 - 1, :],
                                    ALU.add).then_inc(w0_summed, 1)
            dve.wait_ge(w0_summed, 4)
            nc.vector.tensor_copy(w0[:], w0a_sb[:, 0:NT0:4, :]).then_inc(w0_ready, 1)
            dve.wait_ge(w0_hi_ready, 1)
            nc.vector.tensor_tensor(by_three(w0_lo[:]), w0_to_split, by_three(w0_hi[:].bitcast(F32)), ALU.subtract).then_inc(w0_ready, 1)

            def w1_low(c):
                cols = slice(c * CH * N, (c + 1) * CH * N)
                dve.wait_ge(w1_hi_ready, c + 1)
                nc.vector.tensor_tensor(w1_lo[:, cols], stage[c % 2].rearrange("p i n -> p (i n)"), w1_hi[:, cols].bitcast(F32),
                                        ALU.subtract).then_inc(w1_lo_ready, 1)

            for c in range(F // CH):
                w1_low(c)
            for n in range(NT0):
                product(0, n)
            dve.wait_ge(first_x_out, 1)
            for t in range(TILES - 1):
                scalars(t)
            low(0, 0)

            def fold_step(k, t, step):
                par, acc, slot = (t + 1) % 2, acc_d[:, (t + 1) % 2, :], (t - 1) % TILES
                if step == 0:
                    dve.wait_ge(pool_add, adds_done(k, t * ADDS))
                    dve.wait_ge(dve_half, halves_done(k, t * ND))
                    nc.vector.tensor_tensor(acc, acc, acc_p[:, par, :], ALU.add).then_inc(fold, 1)
                elif step == 1:
                    dve.wait_ge(fold, folds_done(k, 3 * t + 1))
                    nc.vector.tensor_tensor(acc[:, 0:2 * N], acc[:, 0:2 * N], acc[:, 2 * N:4 * N], ALU.add).then_inc(fold, 1)
                else:
                    dve.wait_ge(fold, folds_done(k, 3 * t + 2))
                    nc.vector.tensor_tensor(h1[:, slot, :], acc[:, 0:N], acc[:, N:2 * N], ALU.add).then_inc(fold, 1)

            def group(k, q_, block_, layer0):
                for s in range(SLOTS):
                    t, q = s // QUADS, s % QUADS
                    if q - 1 in MIXED:
                        j = DVE_QUADS.index(q - 1)
                        dve.wait_ge(act_quad, act_done(k, t * NA + ACT_QUADS.index(q - 1) + 1))
                        dve.wait_ge(dve_half, halves_done(k, t * ND + j))
                        acc = acc_d[:, t % 2, :]
                        nc.vector.tensor_tensor(acc, acc, tmp[:, tmp_slot(t, ACT_QUADS.index(q - 1)), :], ALU.add).then_inc(dve_half, 2)
                    if q in DVE_QUADS and q not in MIXED:
                        j = DVE_QUADS.index(q)
                        dve.wait_ge(y_ready, k * SLOTS + (s + 1))
                        if j == 0:
                            dve.wait_ge(xs_ready, k * TILES + (t + 1 + LEAD))
                            dve.wait_ge(fold, folds_done(k, 3 * t))
                        for m in range(QUAD):
                            i = q * QUAD + m
                            part, out = yq[:, s % YBANKS, m * N:(m + 1) * N], acc_d[:, t % 2, m * N:(m + 1) * N]
                            if j == 0:
                                ins = nc.vector.tensor_scalar(out, part, xs[:, t, i:i + 1], None, ALU.mult)
                            else:
                                if m % 2 == 0:
                                    dve.wait_ge(dve_half, halves_done(k, t * ND + j - 1) + (m // 2 + 1))
                                ins = nc.vector.scalar_tensor_tensor(out=out, in0=part, scalar=xs[:, t, i:i + 1], in1=out,
                                                                     op0=ALU.mult, op1=ALU.add)
                            if m % 2 == 1:
                                ins.then_inc(dve_half, 1)
                    if s == XS3_SLOT:
                        dve.wait_ge(act_quad, act_done(k, 0))
                        dve.wait_ge(dve_half, halves_done(k, 0))
                        dve.wait_ge(bd_ready, k * TILES + LEAD)
                        scalars(TILES - 1)
                    if s == LOW_SLOT:
                        low(k, 1)
                    if s == SUM_SLOT:
                        sum_depths(k)
                    if q in FOLD_AFTER:
                        if FOLD_AFTER[q] == 2:
                            dve.wait_ge(gx_ready, gx_count(k, block_, 0) if t == 0 else gx_count(k, block_, (3 if layer0 else 2) + t - 1))
                        fold_step(k, t, FOLD_AFTER[q])
                    if layer0:
                        for n in range(NT0):
                            if s == Z_SLOT[n]:
                                product(k + 1, n)
                            if s == ZLO_SLOT[n] and n in SPLIT:
                                z_low(k + 1, n)
                        if t == TILES - 1 and q in COPY_SLOT:
                            c = COPY_SLOT[q]
                            dve.wait_ge(act_quad, act_done(k, (c + 1) * NA))
                            dve.wait_ge(dve_half, halves_done(k, (c + 1) * ND))
                            dve.wait_ge(bd_ready, k * TILES + (c + 1 + LEAD))
                            dve.wait_ge(gx_taken, gx_count(k, block_, 1))
                            scalars(c)
                        if s == LOW0_SLOT:
                            low(k + 1, 0)

            in_loops(dve, group, lambda block_: None)
            dve.wait_ge(gx_ready, GX_END)
            for step in range(3):
                fold_step(GROUPS, 0, step)
            dve.wait_ge(lin3, 1)
            nc.vector.tensor_copy(y_sb, yq[0:1, 0, :]).then_inc(y_in_sbuf, 1)

        @block.tensor
        def _(pe):
            def turn(g, taken):
                pe.wait_ge(xt_in, g * 32 + 32)
                if taken is not None:
                    pe.wait_ge(gx_taken, taken)
                for t in range(TILES):
                    ins = nc.tensor.transpose(gx[:, t * P:(t + 1) * P], rota[:, 0, t * P:(t + 1) * P], ident[:])
                ins.then_inc(gx_ready, 1)

            def contract0(g, n):
                if n == 0 and not (isinstance(g, int) and g == 0):
                    pe.wait_ge(h0_lo_ready, g * 2 + LEAD)
                    pe.wait_ge(h0_summed, g + LEAD)
                if isinstance(g, int) and g == 0:
                    pe.wait_ge(z_ready, n + 1 + LEAD)
                    nc.tensor.matmul(l0acc[:], w0a_sb[:, n, :], z[:, n % ZBUFS, :], start=(n == 0), stop=(n == NT0 - 1)).then_inc(z_used, 1)
                elif n in SPLIT:
                    i = SPLIT.index(n)
                    pe.wait_ge(z_lo_ready, (g - 1) * NSPLIT + (i + 1 + LEAD))
                    nc.tensor.matmul(l0acc[:], w0_hi[:, i, :], z_hi[:, i % ZHBUFS, :], start=False, stop=False)
                    nc.tensor.matmul(l0acc[:], w0_lo[:, i, :], z_hi[:, i % ZHBUFS, :], start=False, stop=False)
                    nc.tensor.matmul(l0acc[:], w0_hi[:, i, :], z_lo[:, i % ZHBUFS, :], start=False, stop=False).then_inc(z_used, 1)
                else:
                    pe.wait_ge(z_ready, g * NT0 + (n + 1 + LEAD))
                    nc.tensor.matmul(l0acc[:], w0[:, n // 4, :], z[:, n % ZBUFS, :],
                                     start=(n == 0), stop=(n == NT0 - 1)).then_inc(z_used, 1)

            def g_product(t):
                nc.tensor.matmul(gx[:], h1[:, (t - 1) % TILES, :], bd[:].rearrange("p s i -> p (s i)"),
                                 start=True, stop=True).then_inc(gx_ready, 1)

            def sum_h1():
                for t in range(TILES):
                    ins = nc.tensor.matmul(gx[:, t * TS:(t + 1) * TS], h1[:, t, :], mask_sb[:], start=True, stop=True)
                ins.then_inc(gx_ready, 1)

            pe.wait_ge(consts_in, 32)
            turn(0, None)
            pe.wait_ge(w0_summed, 4)
            for n in range(NT0):
                contract0(0, n)
            pe.wait_ge(w0_ready, 2)
            pe.wait_ge(w1_lo_ready, F // CH)
            pe.wait_ge(zeroed, 3)
            pe.wait_ge(first_x_out, 1)
            pe.wait_ge(bd_zeroed, 1)

            def group(k, q_, block_, layer0):
                uses = 0
                for s in range(SLOTS):
                    t, q = s // QUADS, s % QUADS
                    if q == 0:
                        pe.wait_ge(h0_lo_ready, k * 2 + (LEAD + (1 if t < TILES - 1 else 2)))
                    before = s - YBANKS
                    if before % QUADS in DVE_QUADS and before % QUADS not in MIXED:
                        pe.wait_ge(dve_half, halves_done(k, quads_before(DVE_QUADS, before + 1)))
                    else:
                        pe.wait_ge(act_quad, act_done(k, quads_before(ACT_QUADS, before + 1)))
                    lhs = slice(t * P, (t + 1) * P)
                    rhs = slice(q * QUAD * N, (q + 1) * QUAD * N)
                    bank = yq[:, s % YBANKS, :]
                    nc.tensor.matmul(bank, h0_hi[:, lhs], w1_hi[:, rhs], start=True, stop=False)
                    nc.tensor.matmul(bank, h0_hi[:, lhs], w1_lo[:, rhs], start=False, stop=False)
                    nc.tensor.matmul(bank, h0_lo[:, lhs], w1_hi[:, rhs], start=False, stop=True).then_inc(y_ready, 1)
                    if layer0:
                        if s == XT_SLOT:
                            turn(k + 1, gx_count(k, block_, uses))
                            uses += 1
                        for n in range(NT0):
                            if s == L0_SLOT[n]:
                                contract0(k + 1, n)
                    if q == G_SLOT:
                        pe.wait_ge(gx_taken, gx_count(k, block_, uses))
                        pe.wait_ge(fold, folds_done(k, 3 * t + 3))
                        pe.wait_ge(bd_ready, k * TILES + (t + LEAD))
                        g_product(t)
                        uses += 1
                    if s == H_SLOT:
                        pe.wait_ge(gx_taken, gx_count(k, block_, uses))
                        sum_h1()
                        uses += 1

            def phase(block_):
                pe.wait_ge(w2_in, 16)
                pe.wait_ge(gx_taken, gx_count(block_ * BLOCK + BLOCK, block_, 0))
                layer2(P)

            def layer2(samples):
                for i in range(F):
                    ins = nc.tensor.matmul(gx[:, 0:samples], w2_sb[:, i, :], gbuf[:, i, 0:samples], start=(i == 0), stop=(i == F - 1))
                ins.then_inc(gx_ready, 1)

            in_loops(pe, group, phase)
            def lin1_term(ms, weight, features, last=False):
                for m in ms:
                    ins = nc.tensor.matmul(yq[:, m, :], weight[:, m * P:(m + 1) * P], features, start=weight is first_weight, stop=last)
                    if last:
                        ins.then_inc(lin1, 1)

            first_weight = wt1_sb[:, 0, :]
            all_m = range(H1 // P)
            pe.wait_ge(weights_in, 16 * 8)
            pe.wait_ge(h0_lo_ready, GROUPS * 2 + LEAD)
            pe.wait_ge(h0_summed, GROUPS + LEAD)
            for c in range(B // P):
                ins = nc.tensor.transpose(l0acc[0:D, c * P:(c + 1) * P], dense_sb[:, c, :], ident[:])
            ins.then_inc(dense_turned, 1)
            pe.wait_ge(dve_half, halves_done(GROUPS, 0))
            pe.wait_ge(act_quad, act_done(GROUPS, 0))
            lin1_term(all_m, first_weight, h0_all)
            pe.wait_ge(gx_taken, GX_END)
            pe.wait_ge(fold, folds_done(GROUPS, 3))
            pe.wait_ge(bd_ready, GROUPS * TILES + LEAD)
            g_product(0)
            pe.wait_ge(dense_ready, 1)
            lin1_term(all_m[:2], wt1d_sb, dense_t)
            pe.wait_ge(gx_taken, GX_END + 1)
            sum_h1()
            lin1_term(all_m[2:], wt1d_sb, dense_t)
            pe.wait_ge(gx_taken, GX_END + 2)
            layer2(P + TS)
            lin1_term(all_m, wt1_sb[:, 1, :], h1sum[:, SAMPLES:])
            pe.wait_ge(gx_taken, GX_END + 3)
            lin1_term(all_m, wt1_sb[:, 2, :], h2sum[:, TS:], last=True)
            for m in range(H2 // P):
                for n in all_m:
                    pe.wait_ge(hid1_ready, n + 1)
                    ins = nc.tensor.matmul(lin2_bank[m][:], wt2_sb[:, n, m * P:(m + 1) * P], hid1[n], start=(n == 0), stop=(n == all_m[-1]))
                ins.then_inc(lin2, 1)
            for m in range(H2 // P):
                pe.wait_ge(hid2_ready, m + 1)
                ins = nc.tensor.matmul(yq[0:1, 0, :], wt3_sb[:, m:m + 1], hid2[m], start=(m == 0), stop=(m == H2 // P - 1))
            ins.then_inc(lin3, 1)


def kernel(**inputs):
    import concourse.bacc as _bacc
    from concourse.bass_utils import run_bass_kernel_spmd as _run

    a = {name: np.ascontiguousarray(x) for name, x in inputs.items()}
    tables = np.concatenate([a[f"tbl_{f}"] for f in range(F)], axis=0)
    starts = np.cumsum([0] + [a[f"tbl_{f}"].shape[0] for f in range(F - 1)]).astype(np.int32)
    id_base = np.repeat(starts.reshape(TILES, D), SAMPLES, axis=0)
    part = np.arange(P)
    shift = np.stack([2 * kb + (part < F) for kb in range(ROTB)], 1)
    first = np.stack([(part + 8 * r) % F for _, r in TILES0], 1)
    second = np.stack([(part - shift[:, kb]) % F for kb, _ in TILES0], 1)
    w0 = a["L0_rec_W0"]
    mask = (part[:, None] // D == np.arange(TS)).astype(np.float32)
    arrays = {
        "tables": tables, "ids": a["ids"], "id_base": id_base, "mask": mask, "eye": np.eye(P, dtype=np.float32),
        "w0a": w0[first * F + second], "w0b": w0[second * F + first], "w1": a["L0_rec_W1"], "w2": a["L0_rec_W2"],
        "dense": a["dense_ctx"], "wt1": a["W_top1"], "bt1": a["b_top1"], "wt2": a["W_top2"], "bt2": a["b_top2"], "wt3": a["W_top3"],
    }
    nc = _bacc.Bacc("TRN2", target_bir_lowering=False, num_devices=1)
    args = [nc.dram_tensor(f"{n}_dram", x.shape, mybir.dt.from_np(x.dtype), kind="ExternalInput").ap() for n, x in arrays.items()]
    args.append(nc.dram_tensor("y_dram", (B, 1), F32, kind="ExternalOutput").ap())
    dlrm(nc, *args)
    r = _run(nc, [{f"{n}_dram": x for n, x in arrays.items()}], core_ids=[0])
    return r.results[0]["y_dram"]
```
